# Optimizing a Trainium2 kernel written in Bass

```python
import numpy as np
import jax
import jax.numpy as jnp

def _softmax(x, axis=-1):
    return jax.nn.softmax(x, axis=axis)

def _gelu(x):
    return jax.nn.gelu(x, approximate=True)

def _silu(x):
    return jax.nn.silu(x)

def _sigmoid(x):
    return jax.nn.sigmoid(x)

def _layernorm(x, axis=-1, eps=1e-05):
    m = jnp.mean(x, axis=axis, keepdims=True)
    v = jnp.var(x, axis=axis, keepdims=True)
    return (x - m) / jnp.sqrt(v + eps)

def _scatter_add(tgt, idx, src, axis=0):
    return tgt.at[idx].add(src)

def _segment_sum(src, seg, n):
    return jax.ops.segment_sum(src, seg, n)
kernel_name = 'mk_adaln_ffn_d1_seqx_r2_6d2b80'

def setup_inputs(seed: int=0):
    np.random.seed(seed)
    _w = jnp.asarray

    def _rec_inputs():
        import jax
        import jax.numpy as jnp
        _rk = jax.random.key(seed)
        x = -1.394e-06 + 0.9999 * jax.random.normal(jax.random.fold_in(_rk, 1), (4, 1024, 1024), jnp.float32)
        _lenS = 1024 - jax.random.randint(jax.random.fold_in(_rk, 7), (4,), 0, max(1, 1024 // 4) + 1, jnp.int32)
        _lenS2 = 1024 - jax.random.randint(jax.random.fold_in(_rk, 8), (4,), 0, max(1, 1024 // 4) + 1, jnp.int32)
        cond_2048 = -0.00499425 + 1.0058 * jax.random.normal(jax.random.fold_in(_rk, 11), (4, 1024), jnp.float32)
        return (x, cond_2048)
    x, cond_2048 = _rec_inputs()

    def _L0_cond_setup():
        import jax, jax.numpy as jnp
        import numpy as np
        B, T, D = (16, 128, 1024)
        key = jax.random.key(seed)
        k0, k1, k2, k3 = jax.random.split(key, 4)
        scale = 1.0 / np.sqrt(D)
        return {'initial_state': jax.random.normal(k0, (B, D), jnp.float32), 'inputs': jax.random.normal(k1, (B, T, D), jnp.float32), 'W_ih': jax.random.normal(k2, (D, 3 * D), jnp.float32) * scale, 'W_hh': jax.random.normal(k3, (D, 3 * D), jnp.float32) * scale, 'b_ih': jnp.zeros((3 * D,), jnp.float32), 'b_hh': jnp.zeros((3 * D,), jnp.float32)}
    _L0_cond_all = _L0_cond_setup()
    _L0_cond_in = {k: v for k, v in _L0_cond_all.items() if k in ('W_ih', 'W_hh', 'b_ih', 'b_hh')}
    del _L0_cond_all

    def _L0_ffn_setup():
        import jax, jax.numpy as jnp
        import numpy as np
        D_MODEL = 1024
        NUM_TILES = 64
        D_SLICE = D_MODEL // NUM_TILES
        TILES_PER_CLUSTER = 8
        NUM_CLUSTERS = NUM_TILES // TILES_PER_CLUSTER
        GRID = 16
        LN_EPS = 1e-05
        DIMS = (np.arange(NUM_TILES)[:, None] * D_SLICE + np.arange(D_SLICE)[None, :]) % D_MODEL
        DIMS = jnp.asarray(DIMS, dtype=jnp.int32)

        def _forward(x, ln_gamma, ln_beta, spline_bases, spline_slopes, output_scale):
            B, S, D = x.shape
            N = B * S
            mu = jnp.mean(x, axis=-1, keepdims=True)
            var = jnp.mean(jnp.square(x - mu), axis=-1, keepdims=True)
            xn = (x - mu) * jax.lax.rsqrt(var + LN_EPS) * ln_gamma + ln_beta
            xf = xn.reshape(N, D)
            slope_sign = jnp.sign(jnp.mean(spline_slopes, axis=-1))
            tile_sigs = jnp.zeros((NUM_TILES, D), dtype=x.dtype)
            tile_sigs = tile_sigs.at[jnp.arange(NUM_TILES)[:, None], DIMS].set(slope_sign)
            cluster_sigs = jnp.sign(tile_sigs.reshape(NUM_CLUSTERS, TILES_PER_CLUSTER, D).mean(axis=1))
            cluster_assign = jnp.arange(NUM_TILES, dtype=jnp.int32) // TILES_PER_CLUSTER
            input_sigs = jnp.sign(xf)
            cluster_scores = input_sigs @ cluster_sigs.T
            best_cluster = jnp.argmax(cluster_scores, axis=-1)
            tile_scores = input_sigs @ tile_sigs.T
            in_cluster = cluster_assign[None, :] == best_cluster[:, None]
            tile_idx = jnp.argmax(jnp.where(in_cluster, tile_scores, -jnp.inf), axis=-1)
            tok_dims = DIMS[tile_idx]
            x_slice = jnp.take_along_axis(xf, tok_dims, axis=1)
            tok_min = x_slice.min(axis=1)
            tok_max = x_slice.max(axis=1)
            onehot = tile_idx[None, :] == jnp.arange(NUM_TILES)[:, None]
            tile_min = jnp.where(onehot, tok_min[None, :], jnp.inf).min(axis=1)
            tile_max = jnp.where(onehot, tok_max[None, :], -jnp.inf).max(axis=1)
            mn = tile_min[tile_idx][:, None]
            mx = tile_max[tile_idx][:, None]
            u = jnp.clip((x_slice - mn) / (mx - mn + 1e-08), 0.0, 1.0 - 1e-06)
            gi = jnp.clip((u * GRID).astype(jnp.int32), 0, GRID - 1)
            j = jnp.arange(D_SLICE)[None, :]
            b = spline_bases[tile_idx[:, None], j, gi]
            s = spline_slopes[tile_idx[:, None], j, gi]
            x_local = (u - gi.astype(u.dtype) / GRID) * GRID
            delta = (b + s * x_local) * output_scale[tile_idx][:, None]
            out = jnp.zeros_like(xf).at[jnp.arange(N)[:, None], tok_dims].set(delta)
            return x + out.reshape(B, S, D)
        key = jax.random.key(seed)
        k1, k2, k3, k4, k5, k6 = jax.random.split(key, 6)
        x = jax.random.normal(k1, (4, 2048, D_MODEL), dtype=jnp.float32)
        ln_gamma = 1.0 + 0.1 * jax.random.normal(k2, (D_MODEL,), dtype=jnp.float32)
        ln_beta = 0.1 * jax.random.normal(k3, (D_MODEL,), dtype=jnp.float32)
        spline_bases = 0.1 * jax.random.normal(k4, (NUM_TILES, D_SLICE, GRID), dtype=jnp.float32)
        spline_slopes = 0.1 + 0.1 * jax.random.normal(k5, (NUM_TILES, D_SLICE, GRID), dtype=jnp.float32)
        output_scale = 1.0 + 0.1 * jax.random.normal(k6, (NUM_TILES,), dtype=jnp.float32)
        return {'x': x, 'ln_gamma': ln_gamma, 'ln_beta': ln_beta, 'spline_bases': spline_bases, 'spline_slopes': spline_slopes, 'output_scale': output_scale}
    _L0_ffn_all = _L0_ffn_setup()
    _L0_ffn_in = {k: v for k, v in _L0_ffn_all.items() if k in ('ln_gamma', 'ln_beta', 'spline_bases', 'spline_slopes', 'output_scale')}
    del _L0_ffn_all
    return {'x': x, 'cond_2048': cond_2048, 'L0_cond_W_ih': _L0_cond_in['W_ih'], 'L0_cond_W_hh': _L0_cond_in['W_hh'], 'L0_cond_b_ih': _L0_cond_in['b_ih'], 'L0_cond_b_hh': _L0_cond_in['b_hh'], 'L0_ffn_ln_gamma': _L0_ffn_in['ln_gamma'], 'L0_ffn_ln_beta': _L0_ffn_in['ln_beta'], 'L0_ffn_spline_bases': _L0_ffn_in['spline_bases'], 'L0_ffn_spline_slopes': _L0_ffn_in['spline_slopes'], 'L0_ffn_output_scale': _L0_ffn_in['output_scale']}

def reference(x, cond_2048, L0_cond_W_ih, L0_cond_W_hh, L0_cond_b_ih, L0_cond_b_hh, L0_ffn_ln_gamma, L0_ffn_ln_beta, L0_ffn_spline_bases, L0_ffn_spline_slopes, L0_ffn_output_scale):
    import jax
    import jax.numpy as jnp

    def _L0_cond_ref(initial_state, inputs, W_ih, W_hh, b_ih, b_hh):
        import jax, jax.numpy as jnp
        import numpy as np
        B, T, D = (16, 128, 1024)
        "ScanOverTime(GRU cell): sequential per-timestep module call with\n            dict-state passing; merge_dict_trees stacks the per-step\n            'state_predicted' tensors along axis=1 -> [B, T, D]."

        def cell(h, x):
            gi = x @ W_ih + b_ih
            gh = h @ W_hh + b_hh
            i_r, i_z, i_n = jnp.split(gi, 3, axis=-1)
            h_r, h_z, h_n = jnp.split(gh, 3, axis=-1)
            r = jax.nn.sigmoid(i_r + h_r)
            z = jax.nn.sigmoid(i_z + h_z)
            n = jnp.tanh(i_n + r * h_n)
            h_new = (1.0 - z) * n + z * h
            return (h_new, h_new)
        xs = jnp.swapaxes(inputs, 0, 1)
        _, hs = jax.lax.scan(cell, initial_state, xs)
        return jnp.swapaxes(hs, 0, 1)

    def _L0_ffn_ref(x, ln_gamma, ln_beta, spline_bases, spline_slopes, output_scale):
        import jax, jax.numpy as jnp
        import numpy as np
        D_MODEL = 1024
        NUM_TILES = 64
        D_SLICE = D_MODEL // NUM_TILES
        TILES_PER_CLUSTER = 8
        NUM_CLUSTERS = NUM_TILES // TILES_PER_CLUSTER
        GRID = 16
        LN_EPS = 1e-05
        DIMS = (np.arange(NUM_TILES)[:, None] * D_SLICE + np.arange(D_SLICE)[None, :]) % D_MODEL
        DIMS = jnp.asarray(DIMS, dtype=jnp.int32)

        def _forward(x, ln_gamma, ln_beta, spline_bases, spline_slopes, output_scale):
            B, S, D = x.shape
            N = B * S
            mu = jnp.mean(x, axis=-1, keepdims=True)
            var = jnp.mean(jnp.square(x - mu), axis=-1, keepdims=True)
            xn = (x - mu) * jax.lax.rsqrt(var + LN_EPS) * ln_gamma + ln_beta
            xf = xn.reshape(N, D)
            slope_sign = jnp.sign(jnp.mean(spline_slopes, axis=-1))
            tile_sigs = jnp.zeros((NUM_TILES, D), dtype=x.dtype)
            tile_sigs = tile_sigs.at[jnp.arange(NUM_TILES)[:, None], DIMS].set(slope_sign)
            cluster_sigs = jnp.sign(tile_sigs.reshape(NUM_CLUSTERS, TILES_PER_CLUSTER, D).mean(axis=1))
            cluster_assign = jnp.arange(NUM_TILES, dtype=jnp.int32) // TILES_PER_CLUSTER
            input_sigs = jnp.sign(xf)
            cluster_scores = input_sigs @ cluster_sigs.T
            best_cluster = jnp.argmax(cluster_scores, axis=-1)
            tile_scores = input_sigs @ tile_sigs.T
            in_cluster = cluster_assign[None, :] == best_cluster[:, None]
            tile_idx = jnp.argmax(jnp.where(in_cluster, tile_scores, -jnp.inf), axis=-1)
            tok_dims = DIMS[tile_idx]
            x_slice = jnp.take_along_axis(xf, tok_dims, axis=1)
            tok_min = x_slice.min(axis=1)
            tok_max = x_slice.max(axis=1)
            onehot = tile_idx[None, :] == jnp.arange(NUM_TILES)[:, None]
            tile_min = jnp.where(onehot, tok_min[None, :], jnp.inf).min(axis=1)
            tile_max = jnp.where(onehot, tok_max[None, :], -jnp.inf).max(axis=1)
            mn = tile_min[tile_idx][:, None]
            mx = tile_max[tile_idx][:, None]
            u = jnp.clip((x_slice - mn) / (mx - mn + 1e-08), 0.0, 1.0 - 1e-06)
            gi = jnp.clip((u * GRID).astype(jnp.int32), 0, GRID - 1)
            j = jnp.arange(D_SLICE)[None, :]
            b = spline_bases[tile_idx[:, None], j, gi]
            s = spline_slopes[tile_idx[:, None], j, gi]
            x_local = (u - gi.astype(u.dtype) / GRID) * GRID
            delta = (b + s * x_local) * output_scale[tile_idx][:, None]
            out = jnp.zeros_like(xf).at[jnp.arange(N)[:, None], tok_dims].set(delta)
            return x + out.reshape(B, S, D)
        return _forward(x, ln_gamma, ln_beta, spline_bases, spline_slopes, output_scale)
    x = x + _L0_ffn_ref(_L0_cond_ref(cond_2048, x, L0_cond_W_ih, L0_cond_W_hh, L0_cond_b_ih, L0_cond_b_hh), L0_ffn_ln_gamma, L0_ffn_ln_beta, L0_ffn_spline_bases, L0_ffn_spline_slopes, L0_ffn_output_scale)
    return x

_drawn_inputs = setup_inputs


def setup_inputs(seed=0):
    import zlib

    import numpy as np

    out = dict(_drawn_inputs(seed))
    spreads = {'L0_cond_b_ih': (0.0, 0.1), 'L0_cond_b_hh': (0.0, 0.1)}
    factors = {'L0_ffn_ln_gamma': 5.184,
     'L0_ffn_ln_beta': 4.385,
     'L0_ffn_spline_bases': 4.708,
     'L0_ffn_spline_slopes': 8.0,
     'L0_ffn_output_scale': 8.0}
    for name, (base, spread) in spreads.items():
        noise = np.random.default_rng([zlib.crc32(name.encode()), seed]).standard_normal(out[name].shape)
        drawn = base * np.exp(spread * noise) if base else spread * noise
        out[name] = jnp.asarray(drawn.astype(out[name].dtype))
    for name, factor in factors.items():
        out[name] = (out[name] * factor).astype(out[name].dtype)
    return out
```

```python
import concourse.bass as bass
from concourse import mybir
from contextlib import ExitStack

F32 = mybir.dt.float32
F16 = mybir.dt.float16
BF16 = mybir.dt.bfloat16
I32 = mybir.dt.int32
ALU = mybir.AluOpType
ACT = mybir.ActivationFunctionType
AX = mybir.AxisListType

BATCH, SEQ, D = 4, 1024, 1024
P = 128
KB = D // P
CHUNKS = 16
LEN = SEQ // CHUNKS
COLS = CHUNKS * BATCH
PAIRS = KB // 2
GW = 6 * COLS
RZ = 4 * COLS
WARM = 44
TILES = LEN // 2
TOKENS = BATCH * SEQ

W_SCALE, S_SCALE = 1024.0, 256.0
UNSCALE = 1.0 / (W_SCALE * S_SCALE)
TOLERANCE = 2.0 ** -20

NT = 64
SLICE = D // NT
GRID = 16
PER_CLUSTER = 8
CLUSTERS = NT // PER_CLUSTER
LN_EPS = 1e-5
BIG = 1e30

NBLK = 8
BW = TOKENS // NBLK
BPOS = BW // COLS
BANKS = 8
MB = 3 * KB


def gate_block(m):
    q, j = divmod(m, 6)
    return q, j, (j // 2) * KB + 2 * q + j % 2


def input_product(nc, ctx, t, W_ih, W_hh, b_ih, b_hh, xT, gi_dram, slopes, gamma, beta, gamma_t, beta_t,
                  out_scale, h0, sign_dram):
    def sb(name, shape, dt=F32):
        return ctx.enter_context(nc.sbuf_tensor(name, shape, dt))

    def sem(name):
        return ctx.enter_context(nc.semaphore(name))

    w_hi, w_lo = t["w_hi"], t["w_lo"]
    wstage = sb("wstage", [P, 2, KB, P])
    xstage = sb("xstage", [P, KB, BW])
    x_hi = sb("x_hi", [P, 2, KB, BW], F16)
    x_lo = sb("x_lo", [P, 2, KB, BW], F16)
    out_stage = sb("out_stage", [P, 2, BPOS, GW])
    bias_i = sb("bias_i", [P, MB])
    bias_h = sb("bias_h", [P, MB])
    bias_gi = sb("bias_gi", [P, MB])
    slope_rows = sb("slope_rows", [NT, SLICE, GRID])
    slope_sum = sb("slope_sum", [NT, SLICE])
    slope_sign = sb("slope_sign", [NT, SLICE])
    sign_b = sb("sign_b", [P, D])
    acc = [ctx.enter_context(nc.psum_tensor(f"acc{i}", [P, BW], F32)) for i in range(BANKS)]

    w_loaded = [sem(f"w_loaded{i}") for i in range(2)]
    x_loaded, x_hi_ready, x_lo_ready = sem("x_loaded"), sem("x_hi_ready"), sem("x_lo_ready")
    w_hi_ready, w_lo_ready = sem("w_hi_ready"), sem("w_lo_ready")
    acc_ready, acc_free = sem("acc_ready"), sem("acc_free")
    gi_stored = [sem(f"gi_stored{i}") for i in range(2)]
    bias_loaded, bias_ready = sem("bias_loaded"), sem("bias_ready")
    slopes_loaded, slopes_summed, sign_ready = sem("slopes_loaded"), sem("slopes_summed"), sem("sign_ready")
    wait_carrier = sem("wait_carrier")
    sign_stored, rows_loaded, rows_ready = sem("sign_stored"), sem("rows_loaded"), sem("rows_ready")

    with nc.Block() as block:

        @block.sync
        def _(sp):
            def load_w(j, src, m):
                if j >= 2:
                    sp.wait_ge(w_hi_ready, j - 1)
                    sp.wait_ge(w_lo_ready, j - 1)
                c = gate_block(m)[2]
                sp.dma_start(wstage[:, j % 2], src.rearrange("(k p) n -> p k n", p=P)[:, :, c * P:(c + 1) * P])\
                  .then_inc(w_loaded[j % 2], 16)

            def load_x(n):
                sp.sem_inc(wait_carrier, 1)
                sp.dma_start(xstage[:], xT.rearrange("(k p) n -> p k n", p=P)[:, :, bass.ds(n * BW, BW)])\
                  .then_inc(x_loaded, 16)

            load_w(0, W_ih, 0)
            load_x(0)
            load_w(1, W_ih, 1)
            sp.dma_start(bias_i[:], b_ih[:]).then_inc(bias_loaded, 16)
            sp.dma_start(bias_h[:], b_hh[:]).then_inc(bias_loaded, 16)
            for m in range(2, MB):
                load_w(m, W_ih, m)
            sp.dma_start(slope_rows[:].rearrange("t j g -> t (j g)"), slopes[:]).then_inc(slopes_loaded, 16)
            sp.dma_start(t["gamma_s"][:], gamma.broadcast_to([P, D])).then_inc(rows_loaded, 16)
            sp.dma_start(t["beta_s"][:], beta.broadcast_to([P, D])).then_inc(rows_loaded, 16)
            for dst, src in ((t["h0"][:], h0), (t["rows"][:, 0:SLICE], gamma_t), (t["rows"][:, SLICE:2 * SLICE], beta_t),
                             (t["rows"][:, ROW_SCALE:ROW_SCALE + 1], out_scale)):
                sp.dma_start(dst, src[:]).then_inc(rows_loaded, 16)
            sp.wait_ge(x_hi_ready, 1)
            sp.wait_ge(x_lo_ready, 1)
            load_x(1)
            sp.wait_ge(sign_ready, 1)
            sp.dma_start(sign_dram[:], slope_sign[:]).then_inc(sign_stored, 16)
            sp.wait_ge(sign_stored, 16)
            sp.dma_start(sign_b[:], sign_dram.rearrange("t j -> (t j)").rearrange("(a n) -> a n", a=1).broadcast_to([P, D]))\
              .then_inc(rows_loaded, 16)
            with sp.Fori(1, NBLK - 1) as n:
                sp.wait_ge(x_hi_ready, n + 1)
                sp.sem_inc(wait_carrier, 1)
                sp.wait_ge(x_lo_ready, n + 1)
                load_x(n + 1)
            for m in range(MB):
                load_w(MB + m, W_hh, m)
            for b in range(2):
                sp.wait_ge(gi_stored[b], 16 * NBLK * PAIRS // 2)
            sp.wait_ge(rows_loaded, 7 * 16)

        def split_w_hi(act, j, m):
            act.wait_ge(w_loaded[j % 2], 16 * (j // 2 + 1))
            c = gate_block(m)[2]
            nc.scalar.activation(w_hi[:, :, c * P:(c + 1) * P], wstage[:, j % 2], ACT.Copy, scale=W_SCALE)\
              .then_inc(w_hi_ready, 1)

        def split_x_hi(act, n, buf):
            act.wait_ge(x_loaded, 16 * (n + 1))
            nc.scalar.activation(x_hi[:, buf], xstage[:], ACT.Copy, scale=S_SCALE).then_inc(x_hi_ready, 1)

        def evict(act, n, m, first):
            q, j, c = gate_block(m)
            act.wait_ge(acc_ready, n * MB + m + 1)
            if j == 0 and not (first and q < 2):
                act.wait_ge(gi_stored[q % 2], n * (16 * PAIRS // 2) + 16 * (q // 2))
            nc.scalar.activation(out_stage[:, q % 2, :, j * COLS:(j + 1) * COLS],
                                 acc[m % BANKS][:].rearrange("p (s c) -> p s c", c=COLS), ACT.Identity,
                                 bias=bias_gi[:, c:c + 1], scale=UNSCALE).then_inc(acc_free, 1)
            if j == 5:
                act.wait_ge(acc_free, n * MB + (BANKS + m + 1))
                act.dma_start(gi_dram[bass.ds(n * BPOS, BPOS), :, q * GW:(q + 1) * GW].rearrange("s p f -> p s f"),
                              out_stage[:, q % 2]).then_inc(gi_stored[q % 2], 16)

        @block.scalar
        def _(act):
            act.sem_inc(acc_free, BANKS)
            split_w_hi(act, 0, 0)
            split_x_hi(act, 0, 0)
            split_w_hi(act, 1, 1)
            split_w_hi(act, 2, 2)
            act.wait_ge(bias_ready, 1)
            for m in range(MB):
                if m + 3 < MB:
                    split_w_hi(act, m + 3, m + 3)
                if m == 20:
                    act.wait_ge(slopes_summed, 1)
                    nc.scalar.activation(slope_sign[:], slope_sum[:], ACT.Sign).then_inc(sign_ready, 1)
                    split_x_hi(act, 1, 1)
                evict(act, 0, m, True)
            with act.Fori(1, NBLK - 1, 2) as n:
                for u in range(2):
                    for m in range(MB):
                        if m == 12:
                            split_x_hi(act, n + u + 1, u)
                        evict(act, n + u, m, False)
            for m in range(MB):
                evict(act, NBLK - 1, m, False)
                split_w_hi(act, MB + m, m)

        def split_w_lo(dve, j, m):
            dve.wait_ge(w_hi_ready, j + 1)
            c = gate_block(m)[2]
            nc.vector.scalar_tensor_tensor(out=w_lo[:, :, c * P:(c + 1) * P], in0=wstage[:, j % 2], scalar=W_SCALE,
                                           in1=w_hi[:, :, c * P:(c + 1) * P], op0=ALU.mult, op1=ALU.subtract)\
              .then_inc(w_lo_ready, 1)

        def split_x_lo(dve, n, buf):
            dve.wait_ge(x_hi_ready, n + 1)
            nc.vector.scalar_tensor_tensor(out=x_lo[:, buf], in0=xstage[:], scalar=S_SCALE, in1=x_hi[:, buf],
                                           op0=ALU.mult, op1=ALU.subtract).then_inc(x_lo_ready, 1)

        @block.vector
        def _(dve):
            split_w_lo(dve, 0, 0)
            split_x_lo(dve, 0, 0)
            split_w_lo(dve, 1, 1)
            dve.wait_ge(bias_loaded, 32)
            nc.vector.tensor_copy(bias_gi[:, 2 * KB:MB], bias_i[:, 2 * KB:MB])
            nc.vector.tensor_scalar(t["bias_hn"][:], bias_h[:, 2 * KB:MB], 1.0 / UNSCALE, None, ALU.mult)
            nc.vector.tensor_tensor(bias_gi[:, 0:2 * KB], bias_i[:, 0:2 * KB], bias_h[:, 0:2 * KB], ALU.add)\
              .then_inc(bias_ready, 1)
            for m in range(2, MB):
                split_w_lo(dve, m, m)
            dve.wait_ge(slopes_loaded, 16)
            nc.vector.tensor_reduce(slope_sum[:], slope_rows[:], AX.X, ALU.add).then_inc(slopes_summed, 1)
            split_x_lo(dve, 1, 1)
            dve.wait_ge(rows_loaded, 7 * 16)
            nc.vector.tensor_tensor(t["gamma_s"][:], t["gamma_s"][:], sign_b[:], ALU.mult)
            nc.vector.tensor_tensor(t["beta_s"][:], t["beta_s"][:], sign_b[:], ALU.mult).then_inc(rows_ready, 1)
            with dve.Fori(1, NBLK - 1, 2) as n:
                for u in range(2):
                    split_x_lo(dve, n + u + 1, u)
            for m in range(MB):
                split_w_lo(dve, MB + m, m)
            nc.vector.memset(t["h"][:, :, 1], 0.0)
            nc.vector.memset(t["hp"][:, 1], 0.0)
            nc.vector.memset(t["flag"][:], 1)

        @block.tensor
        def _(pe):
            with pe.Fori(0, NBLK, 2) as n:
                for u in range(2):
                    pe.wait_ge(x_lo_ready, n + (u + 1))
                    for m in range(MB):
                        pe.wait_ge(w_lo_ready, m + 1)
                        pe.wait_ge(acc_free, n * MB + (u * MB + m + 1))
                        c = gate_block(m)[2]
                        for k in range(KB):
                            hi = w_hi[:, k, c * P:(c + 1) * P]
                            lo = w_lo[:, k, c * P:(c + 1) * P]
                            nc.tensor.matmul(acc[m % BANKS][:], hi, x_hi[:, u, k], start=k == 0, stop=False)
                            nc.tensor.matmul(acc[m % BANKS][:], hi, x_lo[:, u, k], start=False, stop=False)
                            last = nc.tensor.matmul(acc[m % BANKS][:], lo, x_hi[:, u, k], start=False, stop=k == KB - 1)
                        last.then_inc(acc_ready, 1)


REC_X, REC_EXT, REC = NT, NT + SLICE, NT + SLICE + 2
ROW_SCALE, ROW_ID, ROW_EXT, ROW = 2 * SLICE, 2 * SLICE + 1, 2 * SLICE + 2, 2 * SLICE + 4
GROUPS = ((0, 2), (2, 3), (3, 4))
NG = len(GROUPS)


def recurrence(nc, ctx, t, gi_dram, x_rows, y_rows):
    def sb(name, shape, dt=F32):
        return ctx.enter_context(nc.sbuf_tensor(name, shape, dt))

    def pb(name, shape, dt=F32):
        return ctx.enter_context(nc.psum_tensor(name, shape, dt))

    def sem(name):
        return ctx.enter_context(nc.semaphore(name))

    w_hi, w_lo, h, hp, flag = t["w_hi"], t["w_lo"], t["h"], t["hp"], t["flag"]
    gi = sb("gi", [P, 2, PAIRS, GW])
    h_start = sb("h_start", [P, KB, COLS])
    gap_all = sb("gap_all", [P, KB, COLS - BATCH])
    gap = sb("gap", [P, 1])
    gap_over = sb("gap_over", [P, 1])
    rz_sum = sb("rz_sum", [P, PAIRS, RZ])
    rz = sb("rz", [P, PAIRS, RZ])
    rn = sb("rn", [P, PAIRS, 2 * COLS])
    n_sum = sb("n_sum", [P, PAIRS, 2 * COLS])
    n_act = sb("n_act", [P, PAIRS, 2 * COLS])
    diff = sb("diff", [P, PAIRS, 2 * COLS])
    zdiff = sb("zdiff", [P, PAIRS, 2 * COLS])
    x_tile = sb("x_tile", [P, D])
    h_tok = sb("h_tok", [P, D])
    y_tile = sb("y_tile", [P, D])
    xhat = sb("xhat", [P, D])
    scaled = sb("scaled", [P, D])
    signed = sb("signed", [P, D])
    signs = sb("signs", [P, D], BF16)
    stats = sb("stats", [P, 2, 6])
    mean_var = sb("mean_var", [P, 2])
    var_eps = sb("var_eps", [P, 1])
    neg_mean = sb("neg_mean", [P, 1])
    rstd = sb("rstd", [P, 1])
    shift = sb("shift", [P, 1])
    scores = sb("scores", [P, NT])
    cscores = sb("cscores", [P, CLUSTERS])
    ckeys = sb("ckeys", [P, CLUSTERS])
    cbest = sb("cbest", [P, 1])
    chit = sb("chit", [P, CLUSTERS])
    tkeys_in = sb("tkeys_in", [P, NT])
    tkeys = sb("tkeys", [P, NT])
    tbest = sb("tbest", [P, 1])
    hit_t = sb("hit_t", [NT, P])
    record = sb("record", [P, REC])
    x_pick = sb("x_pick", [P, SLICE])
    x_scaled = sb("x_scaled", [P, SLICE])
    miss_big = sb("miss_big", [P, NT])
    cand = sb("cand", [P, 2, NT])

    gates = pb("gates", [P, PAIRS, 512])
    h_turned = pb("h_turned", [P, D])
    hit_bank = pb("hit_bank", [P, 512])
    misc_bank = pb("misc_bank", [P, 512])
    affine = misc_bank[:, 0:2 * SLICE]

    gi_loaded = [sem(f"gi_loaded{i}") for i in range(2)]
    gates_ready, rz_sum_ready, rz_ready, rn_ready, n_sum_ready, n_ready, diff_ready, zdiff_ready, h_ready, head_ready = (
        sem(n) for n in ("gates_ready", "rz_sum_ready", "rz_ready", "rn_ready", "n_sum_ready", "n_ready",
                         "diff_ready", "zdiff_ready", "h_ready", "head_ready"))
    tail_ready = sem("tail_ready")
    start_step, start_copied, start_head, gap_step, gap_ready, gap_summed, pass_judged = (
        sem(n) for n in ("start_step", "start_copied", "start_head", "gap_step", "gap_ready", "gap_summed", "pass_judged"))
    x_loaded, y_ready, y_stored, turned, h_tok_ready, stats_ready, mean_ready, var_ready, rstd_ready, shift_ready = (
        sem(n) for n in ("x_tile_loaded", "y_ready", "y_stored", "turned", "h_tok_ready", "stats_ready", "mean_ready",
                         "var_ready", "rstd_ready", "shift_ready"))
    xhat_ready, scaled_ready, signed_ready, signs_ready, hit_ready, hit_turned, hit_t_ready, affine_ready = (
        sem(n) for n in ("xhat_ready", "scaled_ready", "signed_ready", "signs_ready", "hit_ready", "hit_turned",
                         "hit_t_ready", "affine_ready"))
    wait_carrier = sem("wait_carrier2")
    picked_ready, record_ready, record_kept = sem("picked_ready"), sem("record_ready"), sem("record_kept")
    route_step, slice_step = sem("route_step"), sem("slice_step")
    ROUTE_STEPS, SLICE_STEPS = 8, 9
    picked = scaled

    def groups_before(it, u):
        return it * (2 * NG) + u * NG

    def pair_of(p, i):
        return p * TILES + i + WARM // 2

    def hit_wide():
        return record[:, 0:NT].rearrange("p (t o) -> p t o", o=1).broadcast_to([P, NT, SLICE])

    def sliced(ap):
        return ap[:].rearrange("p (t j) -> p t j", j=SLICE)

    def passes(eng, body):
        with eng.Fori(0, CHUNKS) as p:
            go = eng.value_load(flag[0:1, 0:1], min_val=0, max_val=P)
            with eng.If(go > 0):
                body(p)
                eng.wait_ge(pass_judged, p + 1)
                eng.sem_inc(wait_carrier, 1)

    with nc.Block() as block:

        def pe_pairs(u, pairs, ks):
            src = hp[:, 1 - u]
            for q in pairs:
                out = gates[:, q]
                for k in ks:
                    for j in range(6):
                        c = (j // 2) * KB + 2 * q + j % 2
                        hi, lo = w_hi[:, k, c * P:(c + 1) * P], w_lo[:, k, c * P:(c + 1) * P]
                        o = out[:, j * COLS:(j + 1) * COLS]
                        nc.tensor.matmul(o, hi, src[:, 0, k], start=k == 0 and j == 0, stop=False, skip_group_check=True)
                        nc.tensor.matmul(o, hi, src[:, 1, k], start=False, stop=False, skip_group_check=True)
                        last = nc.tensor.matmul(o, lo, src[:, 0, k], start=False, stop=k == KB - 1, skip_group_check=True)
            return last

        def pe_step(pe, it, seeds, u, after_state=None, after_first=None, after_second=None):
            before = groups_before(it, u)
            pe.wait_ge(tail_ready, before + seeds * NG - 1)
            pe_pairs(u, (0, 1), range(6))
            pe.wait_ge(tail_ready, before + seeds * NG)
            if after_state:
                after_state()
            pe_pairs(u, (0, 1), range(6, KB)).then_inc(gates_ready, 1)
            if after_first:
                after_first()
            pe_pairs(u, (2,), range(KB)).then_inc(gates_ready, 1)
            if after_second:
                after_second()
            pe_pairs(u, (3,), range(KB)).then_inc(gates_ready, 1)

        def pe_turn():
            for k in range(KB):
                ins = nc.tensor.transpose(h_turned[:, k * P:(k + 1) * P], h[:, k].rearrange("p u f -> p (u f)"), t["ident"][:])
            ins.then_inc(turned, 1)

        def pe_hit(pe, T):
            pe.wait_ge(hit_ready, T)
            nc.tensor.transpose(hit_bank[0:REC, 0:P], record[:], t["ident"][:]).then_inc(hit_turned, 1)

        def pe_affine(pe, T):
            pe.wait_ge(hit_t_ready, T)
            nc.tensor.matmul(affine, hit_t[:], t["rows"][:, 0:2 * SLICE], start=True, stop=True).then_inc(affine_ready, 1)

        @block.tensor
        def _(pe):
            with pe.Fori(0, WARM // 2) as it:
                for u in range(2):
                    pe_step(pe, it, 1, u)

            def one_pass(p):
                for u in range(2):
                    pe_step(pe, pair_of(p, 0), p + 2, u)
                with pe.Fori(1, TILES) as i:
                    it, T = pair_of(p, i), p * TILES + i
                    pe_step(pe, it, p + 2, 0, after_state=pe_turn)
                    pe_step(pe, it, p + 2, 1, after_first=lambda: pe_hit(pe, T), after_second=lambda: pe_affine(pe, T))
                pe.wait_ge(tail_ready, groups_before(pair_of(p, TILES), 0) + (p + 2) * NG)
                pe_turn()
                pe_hit(pe, p * TILES + TILES)
                pe_affine(pe, p * TILES + TILES)
                pe.wait_ge(gap_ready, p + 1)
                nc.tensor.matmul(misc_bank[:, 64:65], t["ones"][:], gap_over[:], start=True, stop=True)\
                  .then_inc(gap_summed, 1)

            passes(pe, one_pass)

        def act_group(act, it, u, g):
            a, b = GROUPS[g]
            n = groups_before(it, u) + (g + 1)
            act.wait_ge(rz_sum_ready, n)
            nc.scalar.activation(rz[:, a:b], rz_sum[:, a:b], ACT.Sigmoid).then_inc(rz_ready, 1)
            act.wait_ge(n_sum_ready, n)
            nc.scalar.activation(n_act[:, a:b], n_sum[:, a:b], ACT.Tanh).then_inc(n_ready, 1)
            act.wait_ge(h_ready, n)
            nc.scalar.activation(hp[:, u, 0, 2 * a:2 * b], h[:, 2 * a:2 * b, u], ACT.Copy, scale=S_SCALE)\
              .then_inc(head_ready, 1)

        def act_normalise(act, T):
            act.wait_ge(turned, T)
            act.wait_ge(y_ready, T)
            nc.scalar.activation(h_tok[:], h_turned[:], ACT.Copy).then_inc(h_tok_ready, 1)
            act.wait_ge(shift_ready, T)
            nc.scalar.activation(xhat[:], h_tok[:], ACT.Identity, bias=shift[:], scale=rstd[:]).then_inc(xhat_ready, 1)

        def act_signs(act, T):
            act.wait_ge(signed_ready, T)
            nc.scalar.activation(signs[:], signed[:], ACT.Sign).then_inc(signs_ready, 1)

        def act_hit(act, T):
            act.wait_ge(hit_turned, T)
            nc.scalar.activation(hit_t[:], hit_bank[0:NT, 0:P], ACT.Copy).then_inc(hit_t_ready, 1)

        @block.scalar
        def _(act):
            with act.Fori(0, WARM // 2) as it:
                for u in range(2):
                    for g in range(NG):
                        act_group(act, it, u, g)

            def one_pass(p):
                act.wait_ge(start_copied, p + 1)
                nc.scalar.activation(hp[:, 1, 0], h[:, :, 1], ACT.Copy, scale=S_SCALE).then_inc(start_head, 1)
                for u in range(2):
                    for g in range(NG):
                        act_group(act, pair_of(p, 0), u, g)
                with act.Fori(1, TILES) as i:
                    it, T = pair_of(p, i), p * TILES + i
                    act_normalise(act, T)
                    for g in range(NG):
                        act_group(act, it, 0, g)
                    act_signs(act, T)
                    act_group(act, it, 1, 0)
                    act_hit(act, T)
                    act_group(act, it, 1, 1)
                    act_group(act, it, 1, 2)
                T = p * TILES + TILES
                act_normalise(act, T)
                act_signs(act, T)
                act_hit(act, T)

            passes(act, one_pass)

        def dve_group(dve, it, u, g):
            a, b = GROUPS[g]
            n = groups_before(it, u) + (g + 1)
            dve.wait_ge(gates_ready, n)
            if g == 0:
                dve.wait_ge(gi_loaded[u], it * 16 + 16)
            nc.vector.scalar_tensor_tensor(out=rz_sum[:, a:b], in0=gates[:, a:b, 0:RZ], scalar=UNSCALE,
                                           in1=gi[:, u, a:b, 0:RZ], op0=ALU.mult, op1=ALU.add).then_inc(rz_sum_ready, 1)
            dve.wait_ge(rz_ready, n)
            for q in range(a, b):
                for c in range(2):
                    cols = slice(c * COLS, (c + 1) * COLS)
                    last = nc.vector.scalar_tensor_tensor(
                        out=rn[:, q, cols], in0=gates[:, q, RZ + c * COLS:RZ + (c + 1) * COLS],
                        scalar=t["bias_hn"][:, 2 * q + c:2 * q + c + 1], in1=rz[:, q, cols], op0=ALU.add, op1=ALU.mult)
            last.then_inc(rn_ready, 1)
            dve.wait_ge(rn_ready, n)
            nc.vector.scalar_tensor_tensor(out=n_sum[:, a:b], in0=rn[:, a:b], scalar=UNSCALE, in1=gi[:, u, a:b, RZ:GW],
                                           op0=ALU.mult, op1=ALU.add).then_inc(n_sum_ready, 1)
            dve.wait_ge(n_ready, n)
            old, new = h[:, 2 * a:2 * b, 1 - u], h[:, 2 * a:2 * b, u]

            def blocks(ap):
                return ap[:, a:b].rearrange("p q (c f) -> p (q c) f", c=2)

            nc.vector.tensor_tensor(blocks(diff), old, blocks(n_act), ALU.subtract).then_inc(diff_ready, 1)
            dve.wait_ge(diff_ready, n)
            nc.vector.tensor_tensor(zdiff[:, a:b], rz[:, a:b, 2 * COLS:RZ], diff[:, a:b], ALU.mult).then_inc(zdiff_ready, 1)
            dve.wait_ge(zdiff_ready, n)
            nc.vector.tensor_tensor(new, blocks(n_act), blocks(zdiff), ALU.add).then_inc(h_ready, 1)
            dve.wait_ge(head_ready, n)
            nc.vector.scalar_tensor_tensor(out=hp[:, u, 1, 2 * a:2 * b], in0=h[:, 2 * a:2 * b, u], scalar=S_SCALE,
                                           in1=hp[:, u, 0, 2 * a:2 * b], op0=ALU.mult, op1=ALU.subtract)\
              .then_inc(tail_ready, 1)

        def dve_stats(dve, T):
            dve.wait_ge(h_tok_ready, T)
            for s in range(2):
                nc.vector.bn_stats(stats[:, s], h_tok[:, s * 512:(s + 1) * 512]).then_inc(stats_ready, 1)
            dve.wait_ge(stats_ready, T * 2)
            dve.sem_inc(wait_carrier, 1)
            nc.vector.bn_aggr(mean_var[:], stats[:].rearrange("p a b -> p (a b)")).then_inc(mean_ready, 1)
            dve.wait_ge(mean_ready, T)
            nc.vector.tensor_scalar(var_eps[:], mean_var[:, 1:2], LN_EPS, None, ALU.add)
            nc.vector.tensor_scalar(neg_mean[:], mean_var[:, 0:1], -1.0, None, ALU.mult).then_inc(var_ready, 1)

        def dve_route(dve, T):
            def step(ins, done):
                done[0] += 1
                ins.then_inc(route_step, 1)
                dve.wait_ge(route_step, T * ROUTE_STEPS + (done[0] - ROUTE_STEPS))
                return done[0]

            dve.wait_ge(signs_ready, T)
            done = [0]
            step(nc.vector.tensor_reduce(scores[:], sliced(signs), AX.X, ALU.add), done)
            step(nc.vector.tensor_reduce(cscores[:], scores[:].rearrange("p (c t) -> p c t", t=PER_CLUSTER), AX.X, ALU.add), done)
            step(nc.vector.scalar_tensor_tensor(out=ckeys[:], in0=cscores[:], scalar=float(CLUSTERS), in1=t["cramp"][:],
                                                op0=ALU.mult, op1=ALU.add), done)
            step(nc.vector.tensor_reduce(cbest[:], ckeys[:], AX.X, ALU.max), done)
            step(nc.vector.tensor_scalar(chit[:], ckeys[:], cbest[:], float(8 * NT * SLICE), ALU.is_equal, ALU.mult), done)
            step(nc.vector.scalar_tensor_tensor(out=tkeys_in[:], in0=scores[:], scalar=float(NT), in1=t["tramp"][:],
                                                op0=ALU.mult, op1=ALU.add), done)
            step(nc.vector.tensor_tensor(
                tkeys[:].rearrange("p (c t) -> p c t", t=PER_CLUSTER), tkeys_in[:].rearrange("p (c t) -> p c t", t=PER_CLUSTER),
                chit[:].rearrange("p (c o) -> p c o", o=1).broadcast_to([P, CLUSTERS, PER_CLUSTER]), ALU.add), done)
            assert step(nc.vector.tensor_reduce(tbest[:], tkeys[:], AX.X, ALU.max), done) == ROUTE_STEPS
            nc.vector.tensor_scalar(record[:, 0:NT], tkeys[:], tbest[:], None, ALU.is_equal).then_inc(hit_ready, 1)

        def dve_slice(dve, T):
            def step(ins, done):
                done[0] += 1
                ins.then_inc(slice_step, 1)
                dve.wait_ge(slice_step, T * SLICE_STEPS + (done[0] - SLICE_STEPS))
                return done[0]

            dve.wait_ge(picked_ready, T)
            done = [0]
            step(nc.vector.tensor_reduce(x_pick[:], picked[:].rearrange("p (t j) -> p j t", j=SLICE), AX.X, ALU.add), done)
            dve.wait_ge(affine_ready, T)
            step(nc.vector.tensor_tensor(x_scaled[:], x_pick[:], affine[:, 0:SLICE], ALU.mult), done)
            xs = record[:, REC_X:REC_EXT]
            step(nc.vector.tensor_tensor(xs, x_scaled[:], affine[:, SLICE:2 * SLICE], ALU.add), done)
            lo, hi = record[:, REC_EXT:REC_EXT + 1], record[:, REC_EXT + 1:REC]
            step(nc.vector.tensor_reduce(lo, xs, AX.X, ALU.min), done)
            step(nc.vector.tensor_reduce(hi, xs, AX.X, ALU.max), done)
            step(nc.vector.tensor_scalar(miss_big[:], record[:, 0:NT], 0.0, BIG, ALU.is_equal, ALU.mult), done)
            step(nc.vector.scalar_tensor_tensor(out=cand[:, 0], in0=record[:, 0:NT], scalar=lo, in1=miss_big[:],
                                                op0=ALU.mult, op1=ALU.add), done)
            step(nc.vector.scalar_tensor_tensor(out=cand[:, 1], in0=record[:, 0:NT], scalar=hi, in1=miss_big[:],
                                                op0=ALU.mult, op1=ALU.subtract), done)
            ext = t["extremes"]
            assert step(nc.vector.tensor_tensor(ext[:, 0], ext[:, 0], cand[:, 0], ALU.min), done) == SLICE_STEPS
            nc.vector.tensor_tensor(ext[:, 1], ext[:, 1], cand[:, 1], ALU.max).then_inc(record_ready, 1)

        @block.vector
        def _(dve):
            dve.sem_inc(tail_ready, NG)
            with dve.Fori(0, WARM // 2) as it:
                for u in range(2):
                    for g in range(NG):
                        dve_group(dve, it, u, g)

            def one_pass(p):
                dve.wait_ge(tail_ready, groups_before(pair_of(p, 0), 0) + (p + 1) * NG)
                nc.vector.tensor_copy(h_start[:, :, BATCH:COLS], h[:, :, 1, 0:COLS - BATCH])
                nc.vector.tensor_copy(h_start[:, :, 0:BATCH], t["h0"][:])
                nc.vector.memset(t["extremes"][:, 0], BIG)
                nc.vector.memset(t["extremes"][:, 1], -BIG).then_inc(start_step, 1)
                dve.wait_ge(start_step, p + 1)
                nc.vector.tensor_copy(h[:, :, 1], h_start[:]).then_inc(start_copied, 1)
                dve.wait_ge(start_head, p + 1)
                nc.vector.scalar_tensor_tensor(out=hp[:, 1, 1], in0=h[:, :, 1], scalar=S_SCALE, in1=hp[:, 1, 0],
                                               op0=ALU.mult, op1=ALU.subtract).then_inc(tail_ready, NG)
                for u in range(2):
                    for g in range(NG):
                        dve_group(dve, pair_of(p, 0), u, g)
                with dve.Fori(1, TILES) as i:
                    it, T = pair_of(p, i), p * TILES + i
                    dve_stats(dve, T)
                    for g in range(NG):
                        dve_group(dve, it, 0, g)
                    dve_route(dve, T)
                    for g in range(NG):
                        dve_group(dve, it, 1, g)
                    dve_slice(dve, T)
                T = p * TILES + TILES
                dve_stats(dve, T)
                dve_route(dve, T)
                dve_slice(dve, T)
                nc.vector.tensor_tensor(gap_all[:], h[:, :, 1, 0:COLS - BATCH], h_start[:, :, BATCH:COLS], ALU.subtract)\
                  .then_inc(gap_step, 1)
                dve.wait_ge(gap_step, p * 2 + 1)
                nc.vector.tensor_reduce(gap[:], gap_all[:], AX.XY, ALU.max, apply_absolute_value=True).then_inc(gap_step, 1)
                dve.wait_ge(gap_step, p * 2 + 2)
                nc.vector.tensor_scalar(gap_over[:], gap[:], TOLERANCE, None, ALU.is_gt).then_inc(gap_ready, 1)
                dve.wait_ge(gap_summed, p + 1)
                nc.vector.tensor_copy(flag[:], misc_bank[0:1, 64:65]).then_inc(pass_judged, 1)

            passes(dve, one_pass)

        def pool_tile(pool, T, tile):
            pool.wait_ge(var_ready, T)
            nc.gpsimd.tensor_tensor(rstd[:], var_eps[:], t["neg_half"][:], ALU.pow).then_inc(rstd_ready, 1)
            pool.wait_ge(rstd_ready, T)
            nc.gpsimd.tensor_tensor(shift[:], neg_mean[:], rstd[:], ALU.mult).then_inc(shift_ready, 1)
            pool.wait_ge(xhat_ready, T)
            nc.gpsimd.tensor_tensor(scaled[:], xhat[:], t["gamma_s"][:], ALU.mult).then_inc(scaled_ready, 1)
            pool.wait_ge(scaled_ready, T)
            nc.gpsimd.tensor_tensor(signed[:], scaled[:], t["beta_s"][:], ALU.add).then_inc(signed_ready, 1)
            pool.wait_ge(x_loaded, T * 16)
            pool.wait_ge(y_stored, T * 16)
            nc.gpsimd.tensor_tensor(y_tile[:], h_tok[:], x_tile[:], ALU.add).then_inc(y_ready, 1)
            pool.wait_ge(hit_ready, T)
            nc.gpsimd.tensor_tensor(sliced(picked), sliced(xhat), hit_wide(), ALU.mult).then_inc(picked_ready, 1)
            pool.wait_ge(record_ready, T)
            nc.gpsimd.tensor_copy(t["records"][:, tile], record[:]).then_inc(record_kept, 1)

        @block.gpsimd
        def _(pool):
            pool.sem_inc(y_ready, 1)

            def one_pass(p):
                with pool.Fori(0, TILES) as i:
                    pool_tile(pool, p * TILES + i + 1, i)

            passes(pool, one_pass)

        def load_gi(sp, pos, u):
            sp.dma_start(gi[:, u].rearrange("p q f -> p (q f)"), gi_dram[bass.ds(pos, 1)].rearrange("o p f -> p (o f)"))\
              .then_inc(gi_loaded[u], 16)

        def gi_used(sp, it, u):
            sp.wait_ge(n_sum_ready, groups_before(it, u + 1))
            sp.sem_inc(wait_carrier, 1)

        def load_x(sp, tile):
            sp.dma_start(x_tile[:], x_rows[bass.ds(tile, 1)].rearrange("o p f -> p (o f)")).then_inc(x_loaded, 16)

        def store_y(sp, T, tile):
            sp.wait_ge(y_ready, T + 1)
            sp.sem_inc(wait_carrier, 1)
            sp.dma_start(y_rows[bass.ds(tile, 1)].rearrange("o p f -> p (o f)"), y_tile[:]).then_inc(y_stored, 16)

        @block.sync
        def _(sp):
            sp.sem_inc(y_stored, 16)
            load_gi(sp, LEN - WARM, 0)
            load_gi(sp, LEN - WARM + 1, 1)
            with sp.Fori(0, WARM // 2 - 1) as it:
                for u in range(2):
                    gi_used(sp, it, u)
                    load_gi(sp, it * 2 + (LEN - WARM + 2 + u), u)

            def one_pass(p):
                for u in range(2):
                    gi_used(sp, pair_of(p, -1), u)
                    load_gi(sp, u, u)
                load_x(sp, 0)
                for u in range(2):
                    gi_used(sp, pair_of(p, 0), u)
                    load_gi(sp, 2 + u, u)
                with sp.Fori(1, TILES - 1) as i:
                    it, T = pair_of(p, i), p * TILES + i
                    store_y(sp, T, i - 1)
                    load_x(sp, i)
                    for u in range(2):
                        gi_used(sp, it, u)
                        load_gi(sp, i * 2 + (2 + u), u)
                for i in (TILES - 1, TILES):
                    store_y(sp, p * TILES + i, i - 1)
                    if i < TILES:
                        load_x(sp, i)
                sp.wait_ge(y_stored, p * (TILES * 16) + (TILES + 1) * 16)
                sp.sem_inc(wait_carrier, 1)

            passes(sp, one_pass)


def spline(nc, ctx, t, tables, y_slices):
    def sb(name, shape, dt=F32):
        return ctx.enter_context(nc.sbuf_tensor(name, shape, dt))

    def sem(name):
        return ctx.enter_context(nc.semaphore(name))

    records, rows = t["records"], t["rows"]
    curves = sb("curves", [NT, 2, SLICE * GRID])
    hits_t = sb("hits_t", [NT, TILES, P])
    per_tok = sb("per_tok", [P, TILES, 4])
    span = sb("span", [P, TILES])
    span_eps = sb("span_eps", [P, TILES])
    rspan = sb("rspan", [P, TILES])
    off = sb("off", [P, TILES, SLICE])
    u_raw = sb("u_raw", [P, TILES, SLICE])
    u_clip = sb("u_clip", [P, TILES, SLICE])
    u_grid = sb("u_grid", [P, TILES, SLICE])
    near_i = sb("near_i", [P, TILES, SLICE], I32)
    near = sb("near", [P, TILES, SLICE])
    above = sb("above", [P, TILES, SLICE])
    cell = sb("cell", [P, TILES, SLICE])
    local = sb("local", [P, TILES, SLICE])
    cell_hit = sb("cell_hit", [P, 2, SLICE, GRID])
    chosen = sb("chosen", [P, 2, 2, SLICE, GRID])
    curve = sb("curve", [P, TILES, 2, SLICE])
    rise = sb("rise", [P, TILES, SLICE])
    value = sb("value", [P, TILES, SLICE])
    delta = sb("delta", [P, TILES, SLICE])
    row_f = sb("row_f", [P, TILES])
    row_i = sb("row_i", [P, TILES], I32)

    turn_bank = ctx.enter_context(nc.psum_tensor("turn_bank", [P, 2, 512], F32))
    tok_bank = ctx.enter_context(nc.psum_tensor("tok_bank", [P, 512], F32))
    curve_bank = ctx.enter_context(nc.psum_tensor("curve_bank", [P, 4, 512], F32))

    curves_loaded, ext_turned, ext_ready, hit_turned, hit_copied, tok_ready = (
        sem(n) for n in ("curves_loaded", "ext_turned", "ext_ready", "hit_turned2", "hit_copied", "tok_ready"))
    curve_ready, cell_ready, chosen_ready, curve_used = (sem(n) for n in ("curve_ready", "cell_ready", "chosen_ready", "curve_used"))
    math_step, rows_ready, delta_ready, added = (sem(n) for n in ("math_step", "rows_ready2", "delta_ready", "added"))
    HB = 4
    SETS = 4
    SET = TILES // SETS

    with nc.Block() as block:

        @block.sync
        def _(sp):
            sp.dma_start(curves[:], tables[:]).then_inc(curves_loaded, 16)

        @block.tensor
        def _(pe):
            for e in range(2):
                ins = nc.tensor.transpose(turn_bank[0:NT, 0, e * P:(e + 1) * P], t["extremes"][:, e], t["ident"][:])
            ins.then_inc(ext_turned, 1)
            for s in range(TILES // HB):
                if s == 0:
                    pe.wait_ge(ext_ready, 1)
                if s >= 2:
                    pe.wait_ge(hit_copied, s - 1)
                for i in range(HB):
                    ins = nc.tensor.transpose(turn_bank[0:NT, s % 2, i * P:(i + 1) * P], records[:, s * HB + i, 0:NT], t["ident"][:])
                ins.then_inc(hit_turned, 1)
            pe.wait_ge(hit_copied, TILES // HB)
            for i in range(TILES):
                ins = nc.tensor.matmul(tok_bank[:, i * 4:(i + 1) * 4], hits_t[:, i], rows[:, ROW_SCALE:ROW],
                                       start=True, stop=True)
            ins.then_inc(tok_ready, 1)
            pe.wait_ge(curves_loaded, 16)
            for i in range(TILES):
                if i >= 4:
                    pe.wait_ge(curve_used, i - 3)
                nc.tensor.matmul(curve_bank[:, i % 4], hits_t[:, i], curves[:].rearrange("t a f -> t (a f)"),
                                 start=True, stop=True).then_inc(curve_ready, 1)

        @block.scalar
        def _(act):
            for s in range(TILES // HB):
                act.wait_ge(hit_turned, s + 1)
                nc.scalar.activation(hits_t[:, s * HB:(s + 1) * HB].rearrange("t i p -> t (i p)"), turn_bank[0:NT, s % 2],
                                     ACT.Copy).then_inc(hit_copied, 1)

        @block.vector
        def _(dve):
            done = [0]

            def step(ins):
                done[0] += 1
                ins.then_inc(math_step, 1)
                dve.wait_ge(math_step, done[0])

            dve.wait_ge(ext_turned, 1)
            nc.vector.tensor_reduce(rows[:, ROW_EXT:ROW_EXT + 1], turn_bank[0:NT, 0, 0:P], AX.X, ALU.min)
            nc.vector.tensor_reduce(rows[:, ROW_EXT + 1:ROW], turn_bank[0:NT, 0, P:2 * P], AX.X, ALU.max).then_inc(ext_ready, 1)
            dve.wait_ge(tok_ready, 1)
            step(nc.vector.tensor_copy(per_tok[:], tok_bank[:, 0:4 * TILES].rearrange("p (i f) -> p i f", f=4)))
            scale, tile_id, low, high = (per_tok[:, :, f] for f in range(4))

            def wide(ap):
                return ap.rearrange("p (i o) -> p i o", o=1).broadcast_to([P, TILES, SLICE])

            step(nc.vector.tensor_tensor(row_f[:], tile_id, t["token_row"][:], ALU.add))
            nc.vector.tensor_copy(row_i[:], row_f[:]).then_inc(rows_ready, 1)
            step(nc.vector.tensor_tensor(span[:], high, low, ALU.subtract))
            step(nc.vector.tensor_scalar(span_eps[:], span[:], 1e-8, None, ALU.add))
            step(nc.vector.reciprocal(rspan[:], span_eps[:]))
            step(nc.vector.tensor_tensor(off[:], records[:, :, REC_X:REC_EXT], wide(low), ALU.subtract))
            step(nc.vector.tensor_tensor(u_raw[:], off[:], wide(rspan[:]), ALU.mult))
            step(nc.vector.tensor_scalar(u_clip[:], u_raw[:], 0.0, 1.0 - 1e-6, ALU.max, ALU.min))
            step(nc.vector.tensor_scalar(u_grid[:], u_clip[:], float(GRID), None, ALU.mult))
            step(nc.vector.tensor_copy(near_i[:], u_grid[:]))
            step(nc.vector.tensor_copy(near[:], near_i[:]))
            step(nc.vector.tensor_tensor(above[:], near[:], u_grid[:], ALU.is_gt))
            step(nc.vector.tensor_tensor(cell[:], near[:], above[:], ALU.subtract))
            step(nc.vector.tensor_tensor(local[:], u_grid[:], cell[:], ALU.subtract))
            for i in range(TILES):
                b = i % 2
                nc.vector.tensor_tensor(
                    cell_hit[:, b], cell[:, i].rearrange("p (j o) -> p j o", o=1).broadcast_to([P, SLICE, GRID]),
                    t["grid_ramp"][:].rearrange("p (o g) -> p o g", o=1).broadcast_to([P, SLICE, GRID]), ALU.is_equal)\
                  .then_inc(cell_ready, 1)
                dve.wait_ge(cell_ready, i + 1)
                dve.wait_ge(curve_ready, i + 1)
                hit = cell_hit[:, b].rearrange("p j g -> p (j g)").rearrange("p (o f) -> p o f", o=1)
                nc.vector.tensor_tensor(chosen[:, b].rearrange("p a j g -> p a (j g)"),
                                        curve_bank[:, i % 4].rearrange("p (a f) -> p a f", a=2),
                                        hit.broadcast_to([P, 2, SLICE * GRID]), ALU.mult).then_inc(curve_used, 1)
                dve.wait_ge(curve_used, i + 1)
                step(nc.vector.tensor_reduce(curve[:, i], chosen[:, b], AX.X, ALU.add))
                if (i + 1) % SET == 0:
                    s = slice(i + 1 - SET, i + 1)
                    step(nc.vector.tensor_tensor(rise[:, s], curve[:, s, 1], local[:, s], ALU.mult))
                    step(nc.vector.tensor_tensor(value[:, s], curve[:, s, 0], rise[:, s], ALU.add))
                    nc.vector.tensor_tensor(delta[:, s], value[:, s], wide(scale)[:, s], ALU.mult).then_inc(delta_ready, 1)

        @block.gpsimd
        def _(pool):
            pool.wait_ge(rows_ready, 1)
            for i in range(TILES):
                if i % SET == 0:
                    pool.wait_ge(delta_ready, i // SET + 1)
                pool.indirect_dma_start(out=y_slices[:], out_offset=bass.IndirectOffsetOnAxis(ap=row_i[:, i:i + 1], axis=0),
                                        in_=delta[:, i], in_offset=None, compute_op=ALU.add).then_inc(added, 16)
            pool.wait_ge(added, 16 * TILES)


def constants(nc, t):
    made = t["const_made"]
    with nc.Block() as block:
        @block.gpsimd
        def _(pool):
            nc.gpsimd.memset(t["ident"][:], 0.0).then_inc(made, 1)
            pool.wait_ge(made, 1)
            nc.gpsimd.affine_select(out=t["ident"][:], in_=t["ident"][:], compare_op=ALU.not_equal, fill=1.0, base=0,
                                    pattern=[[-1, P]], channel_multiplier=1)
            nc.gpsimd.memset(t["ones"][:], 1.0)
            nc.gpsimd.memset(t["neg_half"][:], -0.5)
            nc.gpsimd.iota(t["cramp"][:], pattern=[[-1, CLUSTERS]], base=CLUSTERS - 1, channel_multiplier=0,
                           allow_small_or_imprecise_dtypes=True)
            nc.gpsimd.iota(t["tramp"][:], pattern=[[-1, NT]], base=NT - 1, channel_multiplier=0,
                           allow_small_or_imprecise_dtypes=True)
            nc.gpsimd.iota(t["grid_ramp"][:], pattern=[[1, GRID]], base=0, channel_multiplier=0,
                           allow_small_or_imprecise_dtypes=True)
            nc.gpsimd.iota(t["token_row"][:], pattern=[[P * NT, TILES]], base=0, channel_multiplier=NT,
                           allow_small_or_imprecise_dtypes=True)
            nc.gpsimd.iota(t["rows"][:, ROW_ID:ROW_ID + 1], pattern=[[0, 1]], base=0, channel_multiplier=1,
                           allow_small_or_imprecise_dtypes=True)


def program(nc, xT, x_rows, h0, W_ih, W_hh, b_ih, b_hh, gamma, beta, gamma_t, beta_t, slopes, tables, out_scale, y):
    gi_dram = nc.dram_tensor("gi_scratch", [LEN, P, PAIRS * GW], F32, kind="Internal").ap()
    sign_dram = nc.dram_tensor("sign_scratch", [NT, SLICE], F32, kind="Internal").ap()
    with ExitStack() as ctx:
        shapes = {
            "w_hi": ([P, KB, 3 * D], F16), "w_lo": ([P, KB, 3 * D], F16),
            "h": ([P, KB, 2, COLS], F32),
            "hp": ([P, 2, 2, KB, COLS], F16),
            "h0": ([P, KB, BATCH], F32), "flag": ([1, 1], I32), "bias_hn": ([P, KB], F32),
            "gamma_s": ([P, D], F32), "beta_s": ([P, D], F32),
            "ident": ([P, P], F32), "ones": ([P, P], F32), "neg_half": ([P, 1], F32),
            "cramp": ([P, CLUSTERS], F32), "tramp": ([P, NT], F32), "grid_ramp": ([P, GRID], F32),
            "token_row": ([P, TILES], F32), "rows": ([NT, ROW], F32),
        }
        t = {n: ctx.enter_context(nc.sbuf_tensor(n, s, d)) for n, (s, d) in shapes.items()}
        t["const_made"] = ctx.enter_context(nc.semaphore("const_made"))
        constants(nc, t)
        with ExitStack() as phase:
            input_product(nc, phase, t, W_ih, W_hh, b_ih, b_hh, xT, gi_dram, slopes, gamma, beta, gamma_t, beta_t,
                          out_scale, h0, sign_dram)
        t["records"] = ctx.enter_context(nc.sbuf_tensor("records", [P, TILES, REC], F32))
        t["extremes"] = ctx.enter_context(nc.sbuf_tensor("extremes", [P, 2, NT], F32))
        with ExitStack() as phase:
            recurrence(nc, phase, t, gi_dram, x_rows, y.rearrange("(i p) f -> i p f", p=P))
        with ExitStack() as phase:
            spline(nc, phase, t, tables, y.rearrange("r (t j) -> (r t) j", j=SLICE))


def kernel(x, cond_2048, L0_cond_W_ih, L0_cond_W_hh, L0_cond_b_ih, L0_cond_b_hh, L0_ffn_ln_gamma, L0_ffn_ln_beta,
           L0_ffn_spline_bases, L0_ffn_spline_slopes, L0_ffn_output_scale):
    import numpy as np
    import concourse.bacc as bacc
    from concourse.bass_utils import run_bass_kernel_spmd

    def lay(a):
        return np.ascontiguousarray(a)

    x = np.asarray(x)
    steps = x.reshape(BATCH, CHUNKS, LEN, D)
    arrays = {
        "xT": lay(steps.transpose(3, 2, 1, 0).reshape(D, TOKENS)),
        "x_rows": lay(steps.transpose(2, 1, 0, 3).reshape(TILES, P, D)),
        "h0": lay(np.asarray(cond_2048).reshape(BATCH, KB, P).transpose(2, 1, 0)),
        "W_ih": lay(L0_cond_W_ih), "W_hh": lay(L0_cond_W_hh),
        "b_ih": lay(np.asarray(L0_cond_b_ih).reshape(MB, P).T), "b_hh": lay(np.asarray(L0_cond_b_hh).reshape(MB, P).T),
        "gamma": lay(np.asarray(L0_ffn_ln_gamma).reshape(1, D)), "beta": lay(np.asarray(L0_ffn_ln_beta).reshape(1, D)),
        "gamma_t": lay(np.asarray(L0_ffn_ln_gamma).reshape(NT, SLICE)),
        "beta_t": lay(np.asarray(L0_ffn_ln_beta).reshape(NT, SLICE)),
        "slopes": lay(np.asarray(L0_ffn_spline_slopes).reshape(NT, SLICE * GRID)),
        "tables": lay(np.stack([np.asarray(L0_ffn_spline_bases).reshape(NT, -1),
                                np.asarray(L0_ffn_spline_slopes).reshape(NT, -1)], axis=1)),
        "out_scale": lay(np.asarray(L0_ffn_output_scale).reshape(NT, 1)),
    }
    nc = bacc.Bacc("TRN2", target_bir_lowering=False, num_devices=1)
    args = [nc.dram_tensor(f"in_{n}", a.shape, mybir.dt.from_np(a.dtype), kind="ExternalInput").ap() for n, a in arrays.items()]
    y = nc.dram_tensor("y", (TOKENS, D), F32, kind="ExternalOutput").ap()
    program(nc, *args, y)
    got = run_bass_kernel_spmd(nc, [{f"in_{n}": a for n, a in arrays.items()}], core_ids=[0]).results[0]["y"]
    return lay(np.asarray(got).reshape(LEN, CHUNKS, BATCH, D).transpose(2, 1, 0, 3).reshape(BATCH, SEQ, D))
```

```python
import concourse.bass as bass
from concourse import mybir
from contextlib import ExitStack

F32 = mybir.dt.float32
F16 = mybir.dt.float16
BF16 = mybir.dt.bfloat16
I32 = mybir.dt.int32
ALU = mybir.AluOpType
ACT = mybir.ActivationFunctionType
AX = mybir.AxisListType

BATCH, SEQ, D = 4, 1024, 1024
P = 128
KB = D // P
CHUNKS = 16
LEN = SEQ // CHUNKS
COLS = CHUNKS * BATCH
PAIRS = KB // 2
GW = 6 * COLS
RZ = 4 * COLS
WARM_HEADS = 24
WARM_FULL = 20
WARM = WARM_HEADS + WARM_FULL
TILES = LEN // 2
TOKENS = BATCH * SEQ

W_SCALE, S_SCALE = 1024.0, 256.0
UNSCALE = 1.0 / (W_SCALE * S_SCALE)
TOLERANCE = 2.0 ** -20

NT = 64
SLICE = D // NT
GRID = 16
PER_CLUSTER = 8
CLUSTERS = NT // PER_CLUSTER
LN_EPS = 1e-5
BIG = 1e30

NBLK = 8
BW = TOKENS // NBLK
BPOS = BW // COLS
BANKS = 8
MB = 3 * KB


def gate_block(m):
    q, j = divmod(m, 6)
    return q, j, (j // 2) * KB + 2 * q + j % 2


def input_product(nc, ctx, t, W_ih, W_hh, b_ih, b_hh, xT, gi_dram, slopes, gamma, beta, gamma_t, beta_t,
                  out_scale, h0, sign_dram):
    def sb(name, shape, dt=F32):
        return ctx.enter_context(nc.sbuf_tensor(name, shape, dt))

    def sem(name):
        return ctx.enter_context(nc.semaphore(name))

    w_hi, w_lo = t["w_hi"], t["w_lo"]
    wstage = sb("wstage", [P, 2, KB, P])
    xstage = sb("xstage", [P, KB, BW])
    x_hi = sb("x_hi", [P, 2, KB, BW], F16)
    x_lo = sb("x_lo", [P, 2, KB, BW], F16)
    out_stage = sb("out_stage", [P, 2, BPOS, GW])
    bias_i = sb("bias_i", [P, MB])
    bias_h = sb("bias_h", [P, MB])
    bias_gi = sb("bias_gi", [P, MB])
    slope_rows = sb("slope_rows", [NT, SLICE, GRID])
    slope_sum = sb("slope_sum", [NT, SLICE])
    slope_sign = sb("slope_sign", [NT, SLICE])
    sign_b = sb("sign_b", [P, D])
    acc = [ctx.enter_context(nc.psum_tensor(f"acc{i}", [P, BW], F32)) for i in range(BANKS)]

    w_loaded = [sem(f"w_loaded{i}") for i in range(2)]
    x_loaded, x_hi_ready, x_lo_ready = sem("x_loaded"), sem("x_hi_ready"), sem("x_lo_ready")
    w_hi_ready, w_lo_ready = sem("w_hi_ready"), sem("w_lo_ready")
    acc_ready, acc_free = sem("acc_ready"), sem("acc_free")
    gi_stored = [sem(f"gi_stored{i}") for i in range(2)]
    bias_loaded, bias_ready = sem("bias_loaded"), sem("bias_ready")
    slopes_loaded, slopes_summed, sign_ready = sem("slopes_loaded"), sem("slopes_summed"), sem("sign_ready")
    wait_carrier = sem("wait_carrier")
    sign_stored, rows_loaded, rows_ready = sem("sign_stored"), sem("rows_loaded"), sem("rows_ready")

    with nc.Block() as block:

        @block.sync
        def _(sp):
            def load_w(j, src, m):
                if j >= 2:
                    sp.wait_ge(w_hi_ready, j - 1)
                    sp.wait_ge(w_lo_ready, j - 1)
                c = gate_block(m)[2]
                sp.dma_start(wstage[:, j % 2], src.rearrange("(k p) n -> p k n", p=P)[:, :, c * P:(c + 1) * P])\
                  .then_inc(w_loaded[j % 2], 16)

            def load_x(n):
                sp.sem_inc(wait_carrier, 1)
                sp.dma_start(xstage[:], xT.rearrange("(k p) n -> p k n", p=P)[:, :, bass.ds(n * BW, BW)])\
                  .then_inc(x_loaded, 16)

            load_w(0, W_ih, 0)
            load_x(0)
            load_w(1, W_ih, 1)
            sp.dma_start(bias_i[:], b_ih[:]).then_inc(bias_loaded, 16)
            sp.dma_start(bias_h[:], b_hh[:]).then_inc(bias_loaded, 16)
            for m in range(2, MB):
                load_w(m, W_ih, m)
            sp.dma_start(slope_rows[:].rearrange("t j g -> t (j g)"), slopes[:]).then_inc(slopes_loaded, 16)
            sp.dma_start(t["gamma_s"][:], gamma.broadcast_to([P, D])).then_inc(rows_loaded, 16)
            sp.dma_start(t["beta_s"][:], beta.broadcast_to([P, D])).then_inc(rows_loaded, 16)
            for dst, src in ((t["h0"][:], h0), (t["rows"][:, 0:SLICE], gamma_t), (t["rows"][:, SLICE:2 * SLICE], beta_t),
                             (t["rows"][:, ROW_SCALE:ROW_SCALE + 1], out_scale)):
                sp.dma_start(dst, src[:]).then_inc(rows_loaded, 16)
            sp.wait_ge(x_hi_ready, 1)
            sp.wait_ge(x_lo_ready, 1)
            load_x(1)
            sp.wait_ge(sign_ready, 1)
            sp.dma_start(sign_dram[:], slope_sign[:]).then_inc(sign_stored, 16)
            sp.wait_ge(sign_stored, 16)
            sp.dma_start(sign_b[:], sign_dram.rearrange("t j -> (t j)").rearrange("(a n) -> a n", a=1).broadcast_to([P, D]))\
              .then_inc(rows_loaded, 16)
            with sp.Fori(1, NBLK - 1) as n:
                sp.wait_ge(x_hi_ready, n + 1)
                sp.sem_inc(wait_carrier, 1)
                sp.wait_ge(x_lo_ready, n + 1)
                load_x(n + 1)
            for m in range(MB):
                load_w(MB + m, W_hh, m)
            for b in range(2):
                sp.wait_ge(gi_stored[b], 16 * NBLK * PAIRS // 2)
            sp.wait_ge(rows_loaded, 7 * 16)

        def split_w_hi(act, j, m):
            act.wait_ge(w_loaded[j % 2], 16 * (j // 2 + 1))
            c = gate_block(m)[2]
            nc.scalar.activation(w_hi[:, :, c * P:(c + 1) * P], wstage[:, j % 2], ACT.Copy, scale=W_SCALE)\
              .then_inc(w_hi_ready, 1)

        def split_x_hi(act, n, buf):
            act.wait_ge(x_loaded, 16 * (n + 1))
            nc.scalar.activation(x_hi[:, buf], xstage[:], ACT.Copy, scale=S_SCALE).then_inc(x_hi_ready, 1)

        def evict(act, n, m, first):
            q, j, c = gate_block(m)
            act.wait_ge(acc_ready, n * MB + m + 1)
            if j == 0 and not (first and q < 2):
                act.wait_ge(gi_stored[q % 2], n * (16 * PAIRS // 2) + 16 * (q // 2))
            nc.scalar.activation(out_stage[:, q % 2, :, j * COLS:(j + 1) * COLS],
                                 acc[m % BANKS][:].rearrange("p (s c) -> p s c", c=COLS), ACT.Identity,
                                 bias=bias_gi[:, c:c + 1], scale=UNSCALE).then_inc(acc_free, 1)
            if j == 5:
                act.wait_ge(acc_free, n * MB + (BANKS + m + 1))
                act.dma_start(gi_dram[bass.ds(n * BPOS, BPOS), :, q * GW:(q + 1) * GW].rearrange("s p f -> p s f"),
                              out_stage[:, q % 2]).then_inc(gi_stored[q % 2], 16)

        @block.scalar
        def _(act):
            act.sem_inc(acc_free, BANKS)
            split_w_hi(act, 0, 0)
            split_x_hi(act, 0, 0)
            split_w_hi(act, 1, 1)
            split_w_hi(act, 2, 2)
            act.wait_ge(bias_ready, 1)
            for m in range(MB):
                if m + 3 < MB:
                    split_w_hi(act, m + 3, m + 3)
                if m == 20:
                    act.wait_ge(slopes_summed, 1)
                    nc.scalar.activation(slope_sign[:], slope_sum[:], ACT.Sign).then_inc(sign_ready, 1)
                    split_x_hi(act, 1, 1)
                evict(act, 0, m, True)
            with act.Fori(1, NBLK - 1, 2) as n:
                for u in range(2):
                    for m in range(MB):
                        if m == 12:
                            split_x_hi(act, n + u + 1, u)
                        evict(act, n + u, m, False)
            for m in range(MB):
                evict(act, NBLK - 1, m, False)
                split_w_hi(act, MB + m, m)

        def split_w_lo(dve, j, m):
            dve.wait_ge(w_hi_ready, j + 1)
            c = gate_block(m)[2]
            nc.vector.scalar_tensor_tensor(out=w_lo[:, :, c * P:(c + 1) * P], in0=wstage[:, j % 2], scalar=W_SCALE,
                                           in1=w_hi[:, :, c * P:(c + 1) * P], op0=ALU.mult, op1=ALU.subtract)\
              .then_inc(w_lo_ready, 1)

        def split_x_lo(dve, n, buf):
            dve.wait_ge(x_hi_ready, n + 1)
            nc.vector.scalar_tensor_tensor(out=x_lo[:, buf], in0=xstage[:], scalar=S_SCALE, in1=x_hi[:, buf],
                                           op0=ALU.mult, op1=ALU.subtract).then_inc(x_lo_ready, 1)

        @block.vector
        def _(dve):
            split_w_lo(dve, 0, 0)
            split_x_lo(dve, 0, 0)
            split_w_lo(dve, 1, 1)
            dve.wait_ge(bias_loaded, 32)
            nc.vector.tensor_copy(bias_gi[:, 2 * KB:MB], bias_i[:, 2 * KB:MB])
            nc.vector.tensor_copy(t["bias_hn"][:].rearrange("p q (c f) -> p (q c) f", f=COLS),
                                  bias_h[:, 2 * KB:MB].rearrange("p (b o) -> p b o", o=1).broadcast_to([P, KB, COLS]))
            nc.vector.tensor_tensor(bias_gi[:, 0:2 * KB], bias_i[:, 0:2 * KB], bias_h[:, 0:2 * KB], ALU.add)\
              .then_inc(bias_ready, 1)
            for m in range(2, MB):
                split_w_lo(dve, m, m)
            dve.wait_ge(slopes_loaded, 16)
            nc.vector.tensor_reduce(slope_sum[:], slope_rows[:], AX.X, ALU.add).then_inc(slopes_summed, 1)
            split_x_lo(dve, 1, 1)
            dve.wait_ge(rows_loaded, 7 * 16)
            nc.vector.tensor_tensor(t["gamma_s"][:], t["gamma_s"][:], sign_b[:], ALU.mult)
            nc.vector.tensor_tensor(t["beta_s"][:], t["beta_s"][:], sign_b[:], ALU.mult).then_inc(rows_ready, 1)
            with dve.Fori(1, NBLK - 1, 2) as n:
                for u in range(2):
                    split_x_lo(dve, n + u + 1, u)
            for m in range(MB):
                split_w_lo(dve, MB + m, m)
            nc.vector.memset(t["h"][:, :, 1], 0.0)
            nc.vector.memset(t["hp"][:, 1], 0.0)
            nc.vector.memset(t["flag"][:], 1)

        @block.tensor
        def _(pe):
            with pe.Fori(0, NBLK, 2) as n:
                for u in range(2):
                    pe.wait_ge(x_lo_ready, n + (u + 1))
                    for m in range(MB):
                        pe.wait_ge(w_lo_ready, m + 1)
                        pe.wait_ge(acc_free, n * MB + (u * MB + m + 1))
                        c = gate_block(m)[2]
                        for k in range(KB):
                            hi = w_hi[:, k, c * P:(c + 1) * P]
                            lo = w_lo[:, k, c * P:(c + 1) * P]
                            nc.tensor.matmul(acc[m % BANKS][:], hi, x_hi[:, u, k], start=k == 0, stop=False)
                            nc.tensor.matmul(acc[m % BANKS][:], hi, x_lo[:, u, k], start=False, stop=False)
                            last = nc.tensor.matmul(acc[m % BANKS][:], lo, x_hi[:, u, k], start=False, stop=k == KB - 1)
                        last.then_inc(acc_ready, 1)


REC_X, REC_EXT, REC = NT, NT + SLICE, NT + SLICE + 2
ROW_SCALE, ROW_ID, ROW_EXT, ROW = 2 * SLICE, 2 * SLICE + 1, 2 * SLICE + 2, 2 * SLICE + 4
GROUPS = ((0, 2), (2, 3), (3, 4))
NG = len(GROUPS)


def recurrence(nc, ctx, t, gi_dram, x_rows, y_rows):
    def sb(name, shape, dt=F32):
        return ctx.enter_context(nc.sbuf_tensor(name, shape, dt))

    def pb(name, shape, dt=F32):
        return ctx.enter_context(nc.psum_tensor(name, shape, dt))

    def sem(name):
        return ctx.enter_context(nc.semaphore(name))

    w_hi, w_lo, h, hp, flag = t["w_hi"], t["w_lo"], t["h"], t["hp"], t["flag"]
    gi = sb("gi", [P, 2, PAIRS, GW])
    h_start = sb("h_start", [P, KB, COLS])
    gap_all = sb("gap_all", [P, KB, COLS - BATCH])
    gap = sb("gap", [P, 1])
    gap_over = sb("gap_over", [P, 1])
    rz_sum = sb("rz_sum", [P, PAIRS, RZ])
    rz = sb("rz", [P, PAIRS, RZ])
    hn = sb("hn", [P, PAIRS, 2 * COLS])
    rn = sb("rn", [P, PAIRS, 2 * COLS])
    n_sum = sb("n_sum", [P, PAIRS, 2 * COLS])
    n_act = sb("n_act", [P, PAIRS, 2 * COLS])
    not_z = sb("not_z", [P, PAIRS, 2 * COLS])
    z_old = sb("z_old", [P, PAIRS, 2 * COLS])
    new_n = sb("new_n", [P, PAIRS, 2 * COLS])
    x_tile = sb("x_tile", [P, D])
    h_tok = sb("h_tok", [P, D])
    y_tile = sb("y_tile", [P, D])
    xhat = sb("xhat", [P, D])
    scaled = sb("scaled", [P, D])
    signed = sb("signed", [P, D])
    signs = sb("signs", [P, D], BF16)
    stats = sb("stats", [P, 2, 6])
    mean_var = sb("mean_var", [P, 2])
    var_eps = sb("var_eps", [P, 1])
    neg_mean = sb("neg_mean", [P, 1])
    rstd = sb("rstd", [P, 1])
    shift = sb("shift", [P, 1])
    scores = sb("scores", [P, NT])
    cscores = sb("cscores", [P, CLUSTERS])
    ckeys = sb("ckeys", [P, CLUSTERS])
    cbest = sb("cbest", [P, 1])
    chit = sb("chit", [P, CLUSTERS])
    tkeys_in = sb("tkeys_in", [P, NT])
    tkeys = sb("tkeys", [P, NT])
    tbest = sb("tbest", [P, 1])
    hit_t = sb("hit_t", [NT, P])
    record = sb("record", [P, REC])
    x_pick = sb("x_pick", [P, SLICE])
    x_scaled = sb("x_scaled", [P, SLICE])
    miss_big = sb("miss_big", [P, NT])
    cand = sb("cand", [P, 2, NT])

    gates = pb("gates", [P, PAIRS, 512])
    h_turned = pb("h_turned", [P, D])
    hit_bank = pb("hit_bank", [P, 512])
    misc_bank = pb("misc_bank", [P, 512])
    affine = misc_bank[:, 0:2 * SLICE]

    gi_loaded = [sem(f"gi_loaded{i}") for i in range(2)]
    gates_ready, rz_sum_ready, rz_ready, not_z_ready, hn_ready, rn_ready, n_sum_ready, n_ready, z_old_ready, new_n_ready, h_ready = (
        sem(n) for n in ("gates_ready", "rz_sum_ready", "rz_ready", "not_z_ready", "hn_ready", "rn_ready", "n_sum_ready", "n_ready",
                         "z_old_ready", "new_n_ready", "h_ready"))
    head_ready, tail_ready = sem("head_ready"), sem("tail_ready")
    start_step, start_copied, gap_step, gap_ready, gap_summed, pass_judged = (
        sem(n) for n in ("start_step", "start_copied", "gap_step", "gap_ready", "gap_summed", "pass_judged"))
    x_loaded, y_ready, y_stored, turned, h_tok_ready, stats_ready, mean_ready, var_ready, rstd_ready, shift_ready = (
        sem(n) for n in ("x_tile_loaded", "y_ready", "y_stored", "turned", "h_tok_ready", "stats_ready", "mean_ready",
                         "var_ready", "rstd_ready", "shift_ready"))
    xhat_ready, scaled_ready, signed_ready, signs_ready, hit_ready, hit_turned, hit_t_ready, affine_ready = (
        sem(n) for n in ("xhat_ready", "scaled_ready", "signed_ready", "signs_ready", "hit_ready", "hit_turned",
                         "hit_t_ready", "affine_ready"))
    wait_carrier = sem("wait_carrier2")
    picked_ready, record_ready, record_kept, hit_kept = (sem(n) for n in ("picked_ready", "record_ready", "record_kept", "hit_kept"))
    route_step, slice_step = sem("route_step"), sem("slice_step")
    ROUTE_STEPS, SLICE_STEPS = 8, 9
    picked = scaled

    def groups_before(it, u):
        return it * (2 * NG) + u * NG

    def pair_of(p, i):
        return p * TILES + i + WARM // 2

    def hit_wide():
        return record[:, 0:NT].rearrange("p (t o) -> p t o", o=1).broadcast_to([P, NT, SLICE])

    def sliced(ap):
        return ap[:].rearrange("p (t j) -> p t j", j=SLICE)

    def z_share(engine, u, g):
        a, b = GROUPS[g]
        return engine.tensor_tensor(z_old[:, a:b].rearrange("p q (c f) -> p q c f", c=2),
                                    rz[:, a:b, 2 * COLS:RZ].rearrange("p q (c f) -> p q c f", c=2),
                                    h[:, 2 * a:2 * b, 1 - u].rearrange("p (q c) f -> p q c f", c=2), ALU.mult)

    def passes(eng, body):
        with eng.Fori(0, 2) as again:
            with eng.If(eng.value_load(flag[0:1, 0:1], min_val=0, max_val=P) > 0):
                with eng.Fori(0, again * (CHUNKS - 2) + 1) as i:
                    with eng.If(eng.value_load(flag[0:1, 0:1], min_val=0, max_val=P) > 0):
                        p = again + i
                        body(p)
                        eng.wait_ge(pass_judged, p + 1)
                        eng.sem_inc(wait_carrier, 1)

    with nc.Block() as block:

        def pe_pairs(u, pairs, ks, heads_only):
            src = hp[:, 1 - u]
            for q in pairs:
                out = gates[:, q]
                for k in ks:
                    for j in range(6):
                        c = (j // 2) * KB + 2 * q + j % 2
                        hi, lo = w_hi[:, k, c * P:(c + 1) * P], w_lo[:, k, c * P:(c + 1) * P]
                        o = out[:, j * COLS:(j + 1) * COLS]
                        last = nc.tensor.matmul(o, hi, src[:, 0, k], start=k == 0 and j == 0,
                                                stop=heads_only and k == KB - 1, skip_group_check=True)
                        if not heads_only:
                            nc.tensor.matmul(o, hi, src[:, 1, k], start=False, stop=False, skip_group_check=True)
                            last = nc.tensor.matmul(o, lo, src[:, 0, k], start=False, stop=k == KB - 1, skip_group_check=True)
            return last

        def pe_step(pe, it, seeds, u, heads_only=False, after_state=None, after_first=None, after_second=None):
            before = groups_before(it, u) + seeds * NG
            state_ready = head_ready if heads_only else tail_ready
            pe.wait_ge(state_ready, before - 2)
            pe_pairs(u, (0, 1), range(4), heads_only)
            pe.wait_ge(state_ready, before - 1)
            pe_pairs(u, (0, 1), (4, 5), heads_only)
            pe.wait_ge(state_ready, before)
            if after_state:
                after_state()
            pe_pairs(u, (0, 1), (6, 7), heads_only).then_inc(gates_ready, 1)
            if after_first:
                after_first()
            pe_pairs(u, (2,), range(KB), heads_only).then_inc(gates_ready, 1)
            if after_second:
                after_second()
            pe_pairs(u, (3,), range(KB), heads_only).then_inc(gates_ready, 1)

        def pe_turn():
            for k in range(KB):
                ins = nc.tensor.transpose(h_turned[:, k * P:(k + 1) * P], h[:, k].rearrange("p u f -> p (u f)"), t["ident"][:])
            ins.then_inc(turned, 1)

        def pe_hit(pe, T):
            pe.wait_ge(hit_ready, T)
            nc.tensor.transpose(hit_bank[0:REC, 0:P], record[:], t["ident"][:]).then_inc(hit_turned, 1)

        def pe_affine(pe, T):
            pe.wait_ge(hit_t_ready, T)
            nc.tensor.matmul(affine, hit_t[:], t["rows"][:, 0:2 * SLICE], start=True, stop=True).then_inc(affine_ready, 1)

        @block.tensor
        def _(pe):
            with pe.Fori(0, WARM_HEADS // 2) as it:
                for u in range(2):
                    pe_step(pe, it, 1, u, heads_only=True)
            with pe.Fori(WARM_HEADS // 2, WARM // 2) as it:
                for u in range(2):
                    pe_step(pe, it, 1, u)

            def one_pass(p):
                for u in range(2):
                    pe_step(pe, pair_of(p, 0), p + 2, u)
                with pe.Fori(1, TILES) as i:
                    it, T = pair_of(p, i), p * TILES + i
                    pe_step(pe, it, p + 2, 0, after_state=pe_turn)
                    pe_step(pe, it, p + 2, 1, after_first=lambda: pe_hit(pe, T), after_second=lambda: pe_affine(pe, T))
                pe.wait_ge(tail_ready, groups_before(pair_of(p, TILES), 0) + (p + 2) * NG)
                pe_turn()
                pe.wait_ge(gap_ready, p + 1)
                nc.tensor.matmul(misc_bank[:, 64:65], t["ones"][:], gap_over[:], start=True, stop=True)\
                  .then_inc(gap_summed, 1)
                pe_hit(pe, p * TILES + TILES)
                pe_affine(pe, p * TILES + TILES)

            passes(pe, one_pass)

        SPREAD_DVE = "A0 B0 A1 C0 B1 T0 C1 T1 A2 B2 C2 T2".split()
        SPREAD_ACT = "A0 B0 A1 C0 B1 C1 A2 B2 C2".split()
        DENSE_DVE = "A0 B0 A1 C0 B1 A2 C1 B2 C2 T0 T1 T2".split()
        DENSE_ACT = "A0 B0 A1 C0 B1 A2 C1 B2 C2".split()

        def act_stage(act, it, u, stage):
            g = int(stage[1])
            a, b = GROUPS[g]
            n = groups_before(it, u) + (g + 1)
            if stage[0] == "A":
                act.wait_ge(rz_sum_ready, n)
                nc.scalar.activation(rz[:, a:b], rz_sum[:, a:b], ACT.Sigmoid).then_inc(rz_ready, 1)
                nc.scalar.activation(not_z[:, a:b], rz_sum[:, a:b, 2 * COLS:RZ], ACT.Sigmoid, scale=-1.0)\
                  .then_inc(not_z_ready, 1)
            elif stage[0] == "B":
                act.wait_ge(n_sum_ready, n)
                nc.scalar.activation(n_act[:, a:b], n_sum[:, a:b], ACT.Tanh).then_inc(n_ready, 1)
            else:
                act.wait_ge(h_ready, n)
                nc.scalar.activation(hp[:, u, 0, 2 * a:2 * b], h[:, 2 * a:2 * b, u], ACT.Copy, scale=S_SCALE)\
                  .then_inc(head_ready, 1)

        def act_step(act, it, u, order=SPREAD_ACT, after={}):
            for stage in order:
                act_stage(act, it, u, stage)
                if stage in after:
                    after[stage]()

        def act_h_tok(act, T):
            act.wait_ge(turned, T)
            act.wait_ge(y_ready, T)
            nc.scalar.activation(h_tok[:], h_turned[:], ACT.Copy).then_inc(h_tok_ready, 1)

        def act_normalise(act, T):
            act.wait_ge(shift_ready, T)
            nc.scalar.activation(xhat[:], h_tok[:], ACT.Identity, bias=shift[:], scale=rstd[:]).then_inc(xhat_ready, 1)

        def act_signs(act, T):
            act.wait_ge(signed_ready, T)
            nc.scalar.activation(signs[:], signed[:], ACT.Sign).then_inc(signs_ready, 1)

        def act_hit(act, T):
            act.wait_ge(hit_turned, T)
            nc.scalar.activation(hit_t[:], hit_bank[0:NT, 0:P], ACT.Copy).then_inc(hit_t_ready, 1)

        @block.scalar
        def _(act):
            act.sem_inc(head_ready, NG)
            with act.Fori(0, WARM_HEADS // 2) as it:
                for u in range(2):
                    act_step(act, it, u, DENSE_ACT)
            with act.Fori(WARM_HEADS // 2, WARM // 2) as it:
                for u in range(2):
                    act_step(act, it, u)

            def one_pass(p):
                act.wait_ge(start_copied, p + 1)
                nc.scalar.activation(hp[:, 1, 0], h[:, :, 1], ACT.Copy, scale=S_SCALE).then_inc(head_ready, NG)
                for u in range(2):
                    act_step(act, pair_of(p, 0), u)
                with act.Fori(1, TILES) as i:
                    it, T = pair_of(p, i), p * TILES + i
                    act_h_tok(act, T)
                    act_step(act, it, 0, after={"A0": lambda: act_normalise(act, T), "C2": lambda: act_signs(act, T)})
                    act_step(act, it, 1, after={"A0": lambda: act_hit(act, T)})
                T = p * TILES + TILES
                act_h_tok(act, T)
                act_normalise(act, T)
                act_signs(act, T)
                act_hit(act, T)

            passes(act, one_pass)

        def dve_stage(dve, it, seeds, u, stage, z_on_pool):
            g = int(stage[1])
            a, b = GROUPS[g]
            n = groups_before(it, u) + (g + 1)
            h_new = h[:, 2 * a:2 * b, u]

            def blocks(ap):
                return ap[:, a:b].rearrange("p q (c f) -> p (q c) f", c=2)

            if stage[0] == "A":
                dve.wait_ge(gates_ready, n)
                if g == 0:
                    dve.wait_ge(gi_loaded[u], it * 16 + 16)
                nc.vector.scalar_tensor_tensor(out=rz_sum[:, a:b], in0=gates[:, a:b, 0:RZ], scalar=UNSCALE,
                                               in1=gi[:, u, a:b, 0:RZ], op0=ALU.mult, op1=ALU.add).then_inc(rz_sum_ready, 1)
                nc.vector.scalar_tensor_tensor(out=hn[:, a:b], in0=gates[:, a:b, RZ:GW], scalar=UNSCALE,
                                               in1=t["bias_hn"][:, a:b], op0=ALU.mult, op1=ALU.add).then_inc(hn_ready, 1)
            elif stage[0] == "B":
                dve.wait_ge(rz_ready, n)
                dve.wait_ge(hn_ready, n)
                nc.vector.tensor_tensor(rn[:, a:b], hn[:, a:b], rz[:, a:b, 0:2 * COLS], ALU.mult).then_inc(rn_ready, 1)
                dve.wait_ge(rn_ready, n)
                nc.vector.tensor_tensor(n_sum[:, a:b], rn[:, a:b], gi[:, u, a:b, RZ:GW], ALU.add).then_inc(n_sum_ready, 1)
                if not z_on_pool:
                    z_share(nc.vector, u, g).then_inc(z_old_ready, 1)
            elif stage[0] == "C":
                dve.wait_ge(not_z_ready, n)
                dve.wait_ge(n_ready, n)
                nc.vector.tensor_tensor(new_n[:, a:b], not_z[:, a:b], n_act[:, a:b], ALU.mult).then_inc(new_n_ready, 1)
                dve.wait_ge(z_old_ready, n)
                dve.wait_ge(new_n_ready, n)
                nc.vector.tensor_tensor(h_new, blocks(new_n), blocks(z_old), ALU.add).then_inc(h_ready, 1)
            else:
                dve.wait_ge(head_ready, n + seeds * NG)
                nc.vector.scalar_tensor_tensor(out=hp[:, u, 1, 2 * a:2 * b], in0=h_new, scalar=S_SCALE,
                                               in1=hp[:, u, 0, 2 * a:2 * b], op0=ALU.mult, op1=ALU.subtract)\
                  .then_inc(tail_ready, 1)

        def dve_step(dve, it, seeds, u, order=SPREAD_DVE, z_on_pool=False):
            for stage in order:
                dve_stage(dve, it, seeds, u, stage, z_on_pool)

        def dve_stats(dve, T):
            dve.wait_ge(h_tok_ready, T)
            for s in range(2):
                nc.vector.bn_stats(stats[:, s], h_tok[:, s * 512:(s + 1) * 512]).then_inc(stats_ready, 1)
            dve.wait_ge(stats_ready, T * 2)
            dve.sem_inc(wait_carrier, 1)
            nc.vector.bn_aggr(mean_var[:], stats[:].rearrange("p a b -> p (a b)")).then_inc(mean_ready, 1)
            dve.wait_ge(mean_ready, T)
            nc.vector.tensor_scalar(var_eps[:], mean_var[:, 1:2], LN_EPS, None, ALU.add)
            nc.vector.tensor_scalar(neg_mean[:], mean_var[:, 0:1], -1.0, None, ALU.mult).then_inc(var_ready, 1)

        def dve_route(dve, T):
            def step(ins, done):
                done[0] += 1
                ins.then_inc(route_step, 1)
                dve.wait_ge(route_step, T * ROUTE_STEPS + (done[0] - ROUTE_STEPS))
                return done[0]

            dve.wait_ge(signs_ready, T)
            done = [0]
            step(nc.vector.tensor_reduce(scores[:], sliced(signs), AX.X, ALU.add), done)
            step(nc.vector.tensor_reduce(cscores[:], scores[:].rearrange("p (c t) -> p c t", t=PER_CLUSTER), AX.X, ALU.add), done)
            step(nc.vector.scalar_tensor_tensor(out=ckeys[:], in0=cscores[:], scalar=float(CLUSTERS), in1=t["cramp"][:],
                                                op0=ALU.mult, op1=ALU.add), done)
            step(nc.vector.tensor_reduce(cbest[:], ckeys[:], AX.X, ALU.max), done)
            step(nc.vector.tensor_scalar(chit[:], ckeys[:], cbest[:], float(8 * NT * SLICE), ALU.is_equal, ALU.mult), done)
            step(nc.vector.scalar_tensor_tensor(out=tkeys_in[:], in0=scores[:], scalar=float(NT), in1=t["tramp"][:],
                                                op0=ALU.mult, op1=ALU.add), done)
            step(nc.vector.tensor_tensor(
                tkeys[:].rearrange("p (c t) -> p c t", t=PER_CLUSTER), tkeys_in[:].rearrange("p (c t) -> p c t", t=PER_CLUSTER),
                chit[:].rearrange("p (c o) -> p c o", o=1).broadcast_to([P, CLUSTERS, PER_CLUSTER]), ALU.add), done)
            assert step(nc.vector.tensor_reduce(tbest[:], tkeys[:], AX.X, ALU.max), done) == ROUTE_STEPS
            nc.vector.tensor_scalar(record[:, 0:NT], tkeys[:], tbest[:], None, ALU.is_equal).then_inc(hit_ready, 1)

        def dve_slice(dve, T):
            def step(ins, done):
                done[0] += 1
                ins.then_inc(slice_step, 1)
                dve.wait_ge(slice_step, T * SLICE_STEPS + (done[0] - SLICE_STEPS))
                return done[0]

            dve.wait_ge(picked_ready, T)
            done = [0]
            step(nc.vector.tensor_reduce(x_pick[:], picked[:].rearrange("p (t j) -> p j t", j=SLICE), AX.X, ALU.add), done)
            dve.wait_ge(affine_ready, T)
            step(nc.vector.tensor_tensor(x_scaled[:], x_pick[:], affine[:, 0:SLICE], ALU.mult), done)
            xs = record[:, REC_X:REC_EXT]
            step(nc.vector.tensor_tensor(xs, x_scaled[:], affine[:, SLICE:2 * SLICE], ALU.add), done)
            lo, hi = record[:, REC_EXT:REC_EXT + 1], record[:, REC_EXT + 1:REC]
            step(nc.vector.tensor_reduce(lo, xs, AX.X, ALU.min), done)
            step(nc.vector.tensor_reduce(hi, xs, AX.X, ALU.max), done)
            step(nc.vector.tensor_scalar(miss_big[:], record[:, 0:NT], 0.0, BIG, ALU.is_equal, ALU.mult), done)
            step(nc.vector.scalar_tensor_tensor(out=cand[:, 0], in0=record[:, 0:NT], scalar=lo, in1=miss_big[:],
                                                op0=ALU.mult, op1=ALU.add), done)
            step(nc.vector.scalar_tensor_tensor(out=cand[:, 1], in0=record[:, 0:NT], scalar=hi, in1=miss_big[:],
                                                op0=ALU.mult, op1=ALU.subtract), done)
            ext = t["extremes"]
            assert step(nc.vector.tensor_tensor(ext[:, 0], ext[:, 0], cand[:, 0], ALU.min), done) == SLICE_STEPS
            nc.vector.tensor_tensor(ext[:, 1], ext[:, 1], cand[:, 1], ALU.max).then_inc(record_ready, 1)

        @block.vector
        def _(dve):
            dve.sem_inc(tail_ready, NG)
            with dve.Fori(0, WARM_HEADS // 2) as it:
                for u in range(2):
                    dve_step(dve, it, 1, u, DENSE_DVE, z_on_pool=True)
            with dve.Fori(WARM_HEADS // 2, WARM // 2) as it:
                for u in range(2):
                    dve_step(dve, it, 1, u)

            def one_pass(p):
                dve.wait_ge(tail_ready, groups_before(pair_of(p, 0), 0) + (p + 1) * NG)
                nc.vector.tensor_copy(h_start[:, :, BATCH:COLS], h[:, :, 1, 0:COLS - BATCH])
                nc.vector.tensor_copy(h_start[:, :, 0:BATCH], t["h0"][:])
                nc.vector.memset(t["extremes"][:, 0], BIG)
                nc.vector.memset(t["extremes"][:, 1], -BIG).then_inc(start_step, 1)
                dve.wait_ge(start_step, p + 1)
                nc.vector.tensor_copy(h[:, :, 1], h_start[:]).then_inc(start_copied, 1)
                dve.wait_ge(head_ready, groups_before(pair_of(p, 0), 0) + (p + 2) * NG)
                nc.vector.scalar_tensor_tensor(out=hp[:, 1, 1], in0=h[:, :, 1], scalar=S_SCALE, in1=hp[:, 1, 0],
                                               op0=ALU.mult, op1=ALU.subtract).then_inc(tail_ready, NG)
                for u in range(2):
                    dve_step(dve, pair_of(p, 0), p + 2, u)
                with dve.Fori(1, TILES) as i:
                    it, T = pair_of(p, i), p * TILES + i
                    dve_stats(dve, T)
                    dve_step(dve, it, p + 2, 0)
                    dve_route(dve, T)
                    dve_step(dve, it, p + 2, 1)
                    dve_slice(dve, T)
                T = p * TILES + TILES
                dve_stats(dve, T)
                nc.vector.tensor_tensor(gap_all[:], h[:, :, 1, 0:COLS - BATCH], h_start[:, :, BATCH:COLS], ALU.subtract)\
                  .then_inc(gap_step, 1)
                dve.wait_ge(gap_step, p * 2 + 1)
                nc.vector.tensor_reduce(gap[:], gap_all[:], AX.XY, ALU.max, apply_absolute_value=True).then_inc(gap_step, 1)
                dve.wait_ge(gap_step, p * 2 + 2)
                nc.vector.tensor_scalar(gap_over[:], gap[:], TOLERANCE, None, ALU.is_gt).then_inc(gap_ready, 1)
                dve.wait_ge(gap_summed, p + 1)
                nc.vector.tensor_copy(flag[:], misc_bank[0:1, 64:65]).then_inc(pass_judged, 1)
                dve_route(dve, T)
                dve_slice(dve, T)

            passes(dve, one_pass)

        def pool_tile(pool, T, tile):
            pool.wait_ge(var_ready, T)
            nc.gpsimd.tensor_tensor(rstd[:], var_eps[:], t["neg_half"][:], ALU.pow).then_inc(rstd_ready, 1)
            pool.wait_ge(rstd_ready, T)
            nc.gpsimd.tensor_tensor(shift[:], neg_mean[:], rstd[:], ALU.mult).then_inc(shift_ready, 1)
            pool.wait_ge(xhat_ready, T)
            nc.gpsimd.tensor_tensor(scaled[:], xhat[:], t["gamma_s"][:], ALU.mult).then_inc(scaled_ready, 1)
            pool.wait_ge(scaled_ready, T)
            nc.gpsimd.tensor_tensor(signed[:], scaled[:], t["beta_s"][:], ALU.add).then_inc(signed_ready, 1)
            pool.wait_ge(x_loaded, T * 16)
            pool.wait_ge(y_stored, T * 16)
            nc.gpsimd.tensor_tensor(y_tile[:], h_tok[:], x_tile[:], ALU.add).then_inc(y_ready, 1)
            pool.wait_ge(hit_ready, T)
            nc.gpsimd.tensor_tensor(sliced(picked), sliced(xhat), hit_wide(), ALU.mult).then_inc(picked_ready, 1)
            pool.wait_ge(record_ready, T)
            nc.gpsimd.tensor_copy(t["records"][:, tile], record[:, REC_X:REC]).then_inc(record_kept, 1)
            nc.gpsimd.tensor_copy(t["hits_t"][:, tile], hit_t[:]).then_inc(hit_kept, 1)

        @block.gpsimd
        def _(pool):
            pool.sem_inc(y_ready, 1)
            with pool.Fori(0, WARM_HEADS // 2) as it:
                for u in range(2):
                    for g in range(NG):
                        pool.wait_ge(rz_ready, groups_before(it, u) + (g + 1))
                        z_share(nc.gpsimd, u, g).then_inc(z_old_ready, 1)

            def one_pass(p):
                with pool.Fori(0, TILES) as i:
                    pool_tile(pool, p * TILES + i + 1, i)

            passes(pool, one_pass)

        def load_gi(sp, pos, u):
            sp.dma_start(gi[:, u].rearrange("p q f -> p (q f)"), gi_dram[bass.ds(pos, 1)].rearrange("o p f -> p (o f)"))\
              .then_inc(gi_loaded[u], 16)

        def gi_used(sp, it, u):
            sp.wait_ge(n_sum_ready, groups_before(it, u + 1))
            sp.sem_inc(wait_carrier, 1)

        def load_x(sp, tile):
            sp.dma_start(x_tile[:], x_rows[bass.ds(tile, 1)].rearrange("o p f -> p (o f)")).then_inc(x_loaded, 16)

        def store_y(sp, T, tile):
            sp.wait_ge(y_ready, T + 1)
            sp.sem_inc(wait_carrier, 1)
            sp.dma_start(y_rows[bass.ds(tile, 1)].rearrange("o p f -> p (o f)"), y_tile[:]).then_inc(y_stored, 16)

        @block.sync
        def _(sp):
            sp.sem_inc(y_stored, 16)
            load_gi(sp, LEN - WARM, 0)
            load_gi(sp, LEN - WARM + 1, 1)
            with sp.Fori(0, WARM // 2 - 1) as it:
                for u in range(2):
                    gi_used(sp, it, u)
                    load_gi(sp, it * 2 + (LEN - WARM + 2 + u), u)

            def one_pass(p):
                for u in range(2):
                    gi_used(sp, pair_of(p, -1), u)
                    load_gi(sp, u, u)
                load_x(sp, 0)
                for u in range(2):
                    gi_used(sp, pair_of(p, 0), u)
                    load_gi(sp, 2 + u, u)
                with sp.Fori(1, TILES - 1) as i:
                    it, T = pair_of(p, i), p * TILES + i
                    store_y(sp, T, i - 1)
                    load_x(sp, i)
                    for u in range(2):
                        gi_used(sp, it, u)
                        load_gi(sp, i * 2 + (2 + u), u)
                for i in (TILES - 1, TILES):
                    store_y(sp, p * TILES + i, i - 1)
                    if i < TILES:
                        load_x(sp, i)
                sp.wait_ge(y_stored, p * (TILES * 16) + (TILES + 1) * 16)
                sp.sem_inc(wait_carrier, 1)

            passes(sp, one_pass)


def spline(nc, ctx, t, tables, y_slices):
    def sb(name, shape, dt=F32):
        return ctx.enter_context(nc.sbuf_tensor(name, shape, dt))

    def sem(name):
        return ctx.enter_context(nc.semaphore(name))

    records, rows, hits_t = t["records"], t["rows"], t["hits_t"]
    curves = sb("curves", [NT, 2, SLICE * GRID])
    per_tok = sb("per_tok", [P, TILES, 4])
    span = sb("span", [P, TILES])
    span_eps = sb("span_eps", [P, TILES])
    rspan = sb("rspan", [P, TILES])
    off = sb("off", [P, TILES, SLICE])
    u_raw = sb("u_raw", [P, TILES, SLICE])
    u_clip = sb("u_clip", [P, TILES, SLICE])
    u_grid = sb("u_grid", [P, TILES, SLICE])
    near_i = sb("near_i", [P, TILES, SLICE], I32)
    near = sb("near", [P, TILES, SLICE])
    above = sb("above", [P, TILES, SLICE])
    cell = sb("cell", [P, TILES, SLICE])
    local = sb("local", [P, TILES, SLICE])
    RING = 8
    cell_off = sb("cell_off", [P, RING, SLICE, GRID])
    chosen = sb("chosen", [P, 2, 2, SLICE, GRID])
    curve = sb("curve", [P, TILES, 2, SLICE])
    rise = sb("rise", [P, TILES, SLICE])
    value = sb("value", [P, TILES, SLICE])
    delta = sb("delta", [P, TILES, SLICE])
    row_f = sb("row_f", [P, TILES])
    row_i = sb("row_i", [P, TILES], I32)

    turn_bank = ctx.enter_context(nc.psum_tensor("turn_bank", [P, 512], F32))
    tok_bank = ctx.enter_context(nc.psum_tensor("tok_bank", [P, 512], F32))
    curve_bank = ctx.enter_context(nc.psum_tensor("curve_bank", [P, 4, 512], F32))

    curves_loaded, ext_turned, ext_ready, tok_ready = (sem(n) for n in ("curves_loaded", "ext_turned", "ext_ready", "tok_ready"))
    curve_ready, cell_ready, chosen_ready, curve_used = (sem(n) for n in ("curve_ready", "cell_ready", "chosen_ready", "curve_used"))
    math_step, rows_ready, cells_known, delta_ready, added = (
        sem(n) for n in ("math_step", "rows_ready2", "cells_known", "delta_ready", "added"))
    ADD_LAG = 16
    SETS = 4
    SET = TILES // SETS

    with nc.Block() as block:

        @block.sync
        def _(sp):
            sp.dma_start(curves[:], tables[:]).then_inc(curves_loaded, 16)

        @block.tensor
        def _(pe):
            for e in range(2):
                ins = nc.tensor.transpose(turn_bank[0:NT, e * P:(e + 1) * P], t["extremes"][:, e], t["ident"][:])
            ins.then_inc(ext_turned, 1)
            pe.wait_ge(ext_ready, 1)
            for i in range(TILES):
                ins = nc.tensor.matmul(tok_bank[:, i * 4:(i + 1) * 4], hits_t[:, i], rows[:, ROW_SCALE:ROW],
                                       start=True, stop=True)
            ins.then_inc(tok_ready, 1)
            pe.wait_ge(curves_loaded, 16)
            for i in range(TILES):
                if i >= 4:
                    pe.wait_ge(curve_used, i - 3)
                nc.tensor.matmul(curve_bank[:, i % 4], hits_t[:, i], curves[:].rearrange("t a f -> t (a f)"),
                                 start=True, stop=True).then_inc(curve_ready, 1)

        @block.vector
        def _(dve):
            done = [0]

            def step(ins):
                done[0] += 1
                ins.then_inc(math_step, 1)
                dve.wait_ge(math_step, done[0])

            dve.wait_ge(ext_turned, 1)
            nc.vector.tensor_reduce(rows[:, ROW_EXT:ROW_EXT + 1], turn_bank[0:NT, 0:P], AX.X, ALU.min)
            nc.vector.tensor_reduce(rows[:, ROW_EXT + 1:ROW], turn_bank[0:NT, P:2 * P], AX.X, ALU.max).then_inc(ext_ready, 1)
            dve.wait_ge(tok_ready, 1)
            step(nc.vector.tensor_copy(per_tok[:], tok_bank[:, 0:4 * TILES].rearrange("p (i f) -> p i f", f=4)))
            scale, tile_id, low, high = (per_tok[:, :, f] for f in range(4))

            def wide(ap):
                return ap.rearrange("p (i o) -> p i o", o=1).broadcast_to([P, TILES, SLICE])

            step(nc.vector.tensor_tensor(row_f[:], tile_id, t["token_row"][:], ALU.add))
            nc.vector.tensor_copy(row_i[:], row_f[:]).then_inc(rows_ready, 1)
            step(nc.vector.tensor_tensor(span[:], high, low, ALU.subtract))
            step(nc.vector.tensor_scalar(span_eps[:], span[:], 1e-8, None, ALU.add))
            step(nc.vector.reciprocal(rspan[:], span_eps[:]))
            step(nc.vector.tensor_tensor(off[:], records[:, :, 0:SLICE], wide(low), ALU.subtract))
            step(nc.vector.tensor_tensor(u_raw[:], off[:], wide(rspan[:]), ALU.mult))
            step(nc.vector.tensor_scalar(u_clip[:], u_raw[:], 0.0, 1.0 - 1e-6, ALU.max, ALU.min))
            step(nc.vector.tensor_scalar(u_grid[:], u_clip[:], float(GRID), None, ALU.mult))
            step(nc.vector.tensor_copy(near_i[:], u_grid[:]))
            step(nc.vector.tensor_copy(near[:], near_i[:]))
            step(nc.vector.tensor_tensor(above[:], near[:], u_grid[:], ALU.is_gt))
            step(nc.vector.tensor_tensor(cell[:], near[:], above[:], ALU.subtract))
            dve.sem_inc(cells_known, 1)
            step(nc.vector.tensor_tensor(local[:], u_grid[:], cell[:], ALU.subtract))
            for i in range(TILES):
                b = i % 2
                dve.wait_ge(cell_ready, i + 1)
                dve.wait_ge(curve_ready, i + 1)
                away = cell_off[:, i % RING].rearrange("p j g -> p (j g)").rearrange("p (o f) -> p o f", o=1)
                nc.vector.scalar_tensor_tensor(
                    out=chosen[:, b].rearrange("p a j g -> p a (j g)"), in0=away.broadcast_to([P, 2, SLICE * GRID]), scalar=0.0,
                    in1=curve_bank[:, i % 4].rearrange("p (a f) -> p a f", a=2), op0=ALU.is_equal, op1=ALU.mult)\
                  .then_inc(curve_used, 1)
                dve.wait_ge(curve_used, i + 1)
                step(nc.vector.tensor_reduce(curve[:, i], chosen[:, b], AX.X, ALU.add))
                if (i + 1) % SET == 0:
                    s = slice(i + 1 - SET, i + 1)
                    step(nc.vector.tensor_tensor(rise[:, s], curve[:, s, 1], local[:, s], ALU.mult))
                    step(nc.vector.tensor_tensor(value[:, s], curve[:, s, 0], rise[:, s], ALU.add))
                    nc.vector.tensor_tensor(delta[:, s], value[:, s], wide(scale)[:, s], ALU.mult).then_inc(delta_ready, 1)

        def add(pool, i):
            if i % SET == 0:
                pool.wait_ge(delta_ready, i // SET + 1)
            pool.indirect_dma_start(out=y_slices[:], out_offset=bass.IndirectOffsetOnAxis(ap=row_i[:, i:i + 1], axis=0),
                                    in_=delta[:, i], in_offset=None, compute_op=ALU.add).then_inc(added, 16)

        @block.gpsimd
        def _(pool):
            pool.wait_ge(rows_ready, 1)
            pool.wait_ge(cells_known, 1)
            for i in range(TILES):
                if i >= RING:
                    pool.wait_ge(curve_used, i - RING + 1)
                nc.gpsimd.tensor_tensor(
                    cell_off[:, i % RING], cell[:, i].rearrange("p (j o) -> p j o", o=1).broadcast_to([P, SLICE, GRID]),
                    t["grid_ramp"][:].rearrange("p (o g) -> p o g", o=1).broadcast_to([P, SLICE, GRID]), ALU.subtract)\
                  .then_inc(cell_ready, 1)
                if i >= ADD_LAG:
                    add(pool, i - ADD_LAG)
            for i in range(TILES - ADD_LAG, TILES):
                add(pool, i)
            pool.wait_ge(added, 16 * TILES)


def constants(nc, t):
    made = t["const_made"]
    with nc.Block() as block:
        @block.gpsimd
        def _(pool):
            nc.gpsimd.memset(t["ident"][:], 0.0).then_inc(made, 1)
            pool.wait_ge(made, 1)
            nc.gpsimd.affine_select(out=t["ident"][:], in_=t["ident"][:], compare_op=ALU.not_equal, fill=1.0, base=0,
                                    pattern=[[-1, P]], channel_multiplier=1)
            nc.gpsimd.memset(t["ones"][:], 1.0)
            nc.gpsimd.memset(t["neg_half"][:], -0.5)
            nc.gpsimd.iota(t["cramp"][:], pattern=[[-1, CLUSTERS]], base=CLUSTERS - 1, channel_multiplier=0,
                           allow_small_or_imprecise_dtypes=True)
            nc.gpsimd.iota(t["tramp"][:], pattern=[[-1, NT]], base=NT - 1, channel_multiplier=0,
                           allow_small_or_imprecise_dtypes=True)
            nc.gpsimd.iota(t["grid_ramp"][:], pattern=[[1, GRID]], base=0, channel_multiplier=0,
                           allow_small_or_imprecise_dtypes=True)
            nc.gpsimd.iota(t["token_row"][:], pattern=[[P * NT, TILES]], base=0, channel_multiplier=NT,
                           allow_small_or_imprecise_dtypes=True)
            nc.gpsimd.iota(t["rows"][:, ROW_ID:ROW_ID + 1], pattern=[[0, 1]], base=0, channel_multiplier=1,
                           allow_small_or_imprecise_dtypes=True)


def program(nc, xT, x_rows, h0, W_ih, W_hh, b_ih, b_hh, gamma, beta, gamma_t, beta_t, slopes, tables, out_scale, y):
    gi_dram = nc.dram_tensor("gi_scratch", [LEN, P, PAIRS * GW], F32, kind="Internal").ap()
    sign_dram = nc.dram_tensor("sign_scratch", [NT, SLICE], F32, kind="Internal").ap()
    with ExitStack() as ctx:
        shapes = {
            "w_hi": ([P, KB, 3 * D], F16), "w_lo": ([P, KB, 3 * D], F16),
            "h": ([P, KB, 2, COLS], F32),
            "hp": ([P, 2, 2, KB, COLS], F16),
            "h0": ([P, KB, BATCH], F32), "flag": ([1, 1], I32), "bias_hn": ([P, PAIRS, 2 * COLS], F32),
            "gamma_s": ([P, D], F32), "beta_s": ([P, D], F32),
            "ident": ([P, P], F32), "ones": ([P, P], F32), "neg_half": ([P, 1], F32),
            "cramp": ([P, CLUSTERS], F32), "tramp": ([P, NT], F32), "grid_ramp": ([P, GRID], F32),
            "token_row": ([P, TILES], F32), "rows": ([NT, ROW], F32),
        }
        t = {n: ctx.enter_context(nc.sbuf_tensor(n, s, d)) for n, (s, d) in shapes.items()}
        t["const_made"] = ctx.enter_context(nc.semaphore("const_made"))
        constants(nc, t)
        with ExitStack() as phase:
            input_product(nc, phase, t, W_ih, W_hh, b_ih, b_hh, xT, gi_dram, slopes, gamma, beta, gamma_t, beta_t,
                          out_scale, h0, sign_dram)
        t["records"] = ctx.enter_context(nc.sbuf_tensor("records", [P, TILES, REC - REC_X], F32))
        t["hits_t"] = ctx.enter_context(nc.sbuf_tensor("hits_t", [NT, TILES, P], F32))
        t["extremes"] = ctx.enter_context(nc.sbuf_tensor("extremes", [P, 2, NT], F32))
        with ExitStack() as phase:
            recurrence(nc, phase, t, gi_dram, x_rows, y.rearrange("(i p) f -> i p f", p=P))
        with ExitStack() as phase:
            spline(nc, phase, t, tables, y.rearrange("r (t j) -> (r t) j", j=SLICE))


def kernel(x, cond_2048, L0_cond_W_ih, L0_cond_W_hh, L0_cond_b_ih, L0_cond_b_hh, L0_ffn_ln_gamma, L0_ffn_ln_beta,
           L0_ffn_spline_bases, L0_ffn_spline_slopes, L0_ffn_output_scale):
    import numpy as np
    import concourse.bacc as bacc
    from concourse.bass_utils import run_bass_kernel_spmd

    def lay(a):
        return np.ascontiguousarray(a)

    x = np.asarray(x)
    steps = x.reshape(BATCH, CHUNKS, LEN, D)
    arrays = {
        "xT": lay(steps.transpose(3, 2, 1, 0).reshape(D, TOKENS)),
        "x_rows": lay(steps.transpose(2, 1, 0, 3).reshape(TILES, P, D)),
        "h0": lay(np.asarray(cond_2048).reshape(BATCH, KB, P).transpose(2, 1, 0)),
        "W_ih": lay(L0_cond_W_ih), "W_hh": lay(L0_cond_W_hh),
        "b_ih": lay(np.asarray(L0_cond_b_ih).reshape(MB, P).T), "b_hh": lay(np.asarray(L0_cond_b_hh).reshape(MB, P).T),
        "gamma": lay(np.asarray(L0_ffn_ln_gamma).reshape(1, D)), "beta": lay(np.asarray(L0_ffn_ln_beta).reshape(1, D)),
        "gamma_t": lay(np.asarray(L0_ffn_ln_gamma).reshape(NT, SLICE)),
        "beta_t": lay(np.asarray(L0_ffn_ln_beta).reshape(NT, SLICE)),
        "slopes": lay(np.asarray(L0_ffn_spline_slopes).reshape(NT, SLICE * GRID)),
        "tables": lay(np.stack([np.asarray(L0_ffn_spline_bases).reshape(NT, -1),
                                np.asarray(L0_ffn_spline_slopes).reshape(NT, -1)], axis=1)),
        "out_scale": lay(np.asarray(L0_ffn_output_scale).reshape(NT, 1)),
    }
    nc = bacc.Bacc("TRN2", target_bir_lowering=False, num_devices=1)
    args = [nc.dram_tensor(f"in_{n}", a.shape, mybir.dt.from_np(a.dtype), kind="ExternalInput").ap() for n, a in arrays.items()]
    y = nc.dram_tensor("y", (TOKENS, D), F32, kind="ExternalOutput").ap()
    program(nc, *args, y)
    got = run_bass_kernel_spmd(nc, [{f"in_{n}": a for n, a in arrays.items()}], core_ids=[0]).results[0]["y"]
    return lay(np.asarray(got).reshape(LEN, CHUNKS, BATCH, D).transpose(2, 1, 0, 3).reshape(BATCH, SEQ, D))
```

```python
import concourse.bass as bass
from concourse import mybir
from contextlib import ExitStack

F32 = mybir.dt.float32
F16 = mybir.dt.float16
BF16 = mybir.dt.bfloat16
I32 = mybir.dt.int32
ALU = mybir.AluOpType
ACT = mybir.ActivationFunctionType
AX = mybir.AxisListType

BATCH, SEQ, D = 4, 1024, 1024
P = 128
KB = D // P
CHUNKS = 16
LEN = SEQ // CHUNKS
COLS = CHUNKS * BATCH
PAIRS = KB // 2
GW = 6 * COLS
RZ = 4 * COLS
WARM_HEADS = 24
WARM_FULL = 20
WARM = WARM_HEADS + WARM_FULL
TILES = LEN // 2
TOKENS = BATCH * SEQ

W_SCALE, S_SCALE = 1024.0, 256.0
UNSCALE = 1.0 / (W_SCALE * S_SCALE)
TOLERANCE = 2.0 ** -20
DIFF_BOUND = 2.0 ** -8
DIFF_FROM = LEN - WARM_FULL
DIFF_TILE = DIFF_FROM // 2

NT = 64
SLICE = D // NT
GRID = 16
PER_CLUSTER = 8
CLUSTERS = NT // PER_CLUSTER
LN_EPS = 1e-5
BIG = 1e30

NBLK = 8
BW = TOKENS // NBLK
BPOS = BW // COLS
BANKS = 8
KX = 2
XPARTS = KB // KX
MB = 3 * KB


def gate_block(m):
    q, j = divmod(m, 6)
    return q, j, (j // 2) * KB + 2 * q + j % 2


def input_product(nc, ctx, t, W_ih, W_hh, b_ih, b_hh, xT, gi_dram, slopes, gamma, beta, gamma_t, beta_t,
                  out_scale, h0, sign_dram):
    def sb(name, shape, dt=F32):
        return ctx.enter_context(nc.sbuf_tensor(name, shape, dt))

    def sem(name):
        return ctx.enter_context(nc.semaphore(name))

    w_hi, w_lo = t["w_hi"], t["w_lo"]
    wstage = sb("wstage", [P, 2, KB, P])
    xstage = sb("xstage", [P, KB, BW])
    x_hi = sb("x_hi", [P, 2, KB, BW], F16)
    x_lo = sb("x_lo", [P, 2, KB, BW], F16)
    out_stage = sb("out_stage", [P, 2, BPOS, GW])
    bias_i = sb("bias_i", [P, MB])
    bias_h = sb("bias_h", [P, MB])
    bias_gi = sb("bias_gi", [P, MB])
    slope_rows = sb("slope_rows", [NT, SLICE, GRID])
    slope_sum = sb("slope_sum", [NT, SLICE])
    slope_sign = sb("slope_sign", [NT, SLICE])
    sign_b = sb("sign_b", [P, D])
    acc = [ctx.enter_context(nc.psum_tensor(f"acc{i}", [P, BW], F32)) for i in range(BANKS)]

    w_loaded = [sem(f"w_loaded{i}") for i in range(2)]
    x_loaded = [sem(f"x_loaded{i}") for i in range(XPARTS)]
    x_hi_ready, x_lo_ready = sem("x_hi_ready"), sem("x_lo_ready")
    w_hi_ready, w_lo_ready = sem("w_hi_ready"), sem("w_lo_ready")
    acc_ready, acc_free = sem("acc_ready"), sem("acc_free")
    gi_stored = [sem(f"gi_stored{i}") for i in range(2)]
    bias_loaded, bias_ready = sem("bias_loaded"), sem("bias_ready")
    slopes_loaded, slopes_summed, sign_ready = sem("slopes_loaded"), sem("slopes_summed"), sem("sign_ready")
    wait_carrier = sem("wait_carrier")
    sign_stored, rows_loaded, rows_ready = sem("sign_stored"), sem("rows_loaded"), sem("rows_ready")

    with nc.Block() as block:

        @block.sync
        def _(sp):
            def load_w(j, src, m):
                if j >= 2:
                    sp.wait_ge(w_hi_ready, j - 1)
                    sp.wait_ge(w_lo_ready, j - 1)
                c = gate_block(m)[2]
                sp.dma_start(wstage[:, j % 2], src.rearrange("(k p) n -> p k n", p=P)[:, :, c * P:(c + 1) * P])\
                  .then_inc(w_loaded[j % 2], 16)

            def load_x(n):
                sp.sem_inc(wait_carrier, 1)
                for k in range(0, KB, KX):
                    sp.dma_start(xstage[:, k:k + KX], xT.rearrange("(k p) n -> p k n", p=P)[:, k:k + KX, bass.ds(n * BW, BW)])\
                      .then_inc(x_loaded[k // KX], 16)

            load_w(0, W_ih, 0)
            load_x(0)
            load_w(1, W_ih, 1)
            sp.dma_start(bias_i[:], b_ih[:]).then_inc(bias_loaded, 16)
            sp.dma_start(bias_h[:], b_hh[:]).then_inc(bias_loaded, 16)
            for m in range(2, MB):
                load_w(m, W_ih, m)
            sp.dma_start(slope_rows[:].rearrange("t j g -> t (j g)"), slopes[:]).then_inc(slopes_loaded, 16)
            sp.dma_start(t["gamma_s"][:], gamma.broadcast_to([P, D])).then_inc(rows_loaded, 16)
            sp.dma_start(t["beta_s"][:], beta.broadcast_to([P, D])).then_inc(rows_loaded, 16)
            for dst, src in ((t["h0"][:], h0), (t["rows"][:, 0:SLICE], gamma_t), (t["rows"][:, SLICE:2 * SLICE], beta_t),
                             (t["rows"][:, ROW_SCALE:ROW_SCALE + 1], out_scale)):
                sp.dma_start(dst, src[:]).then_inc(rows_loaded, 16)
            sp.wait_ge(x_hi_ready, XPARTS)
            sp.wait_ge(x_lo_ready, XPARTS)
            load_x(1)
            sp.wait_ge(sign_ready, 1)
            sp.dma_start(sign_dram[:], slope_sign[:]).then_inc(sign_stored, 16)
            sp.wait_ge(sign_stored, 16)
            sp.dma_start(sign_b[:], sign_dram.rearrange("t j -> (t j)").rearrange("(a n) -> a n", a=1).broadcast_to([P, D]))\
              .then_inc(rows_loaded, 16)
            with sp.Fori(1, NBLK - 1) as n:
                sp.wait_ge(x_hi_ready, n * XPARTS + XPARTS)
                sp.sem_inc(wait_carrier, 1)
                sp.wait_ge(x_lo_ready, n * XPARTS + XPARTS)
                load_x(n + 1)
            for m in range(MB):
                load_w(MB + m, W_hh, m)
            for b in range(2):
                sp.wait_ge(gi_stored[b], 16 * NBLK * PAIRS // 2)
            sp.wait_ge(rows_loaded, 7 * 16)

        def split_w_hi(act, j, m):
            act.wait_ge(w_loaded[j % 2], 16 * (j // 2 + 1))
            c = gate_block(m)[2]
            nc.scalar.activation(w_hi[:, :, c * P:(c + 1) * P], wstage[:, j % 2], ACT.Copy, scale=W_SCALE)\
              .then_inc(w_hi_ready, 1)

        def split_x_hi(act, n, buf):
            for k in range(0, KB, KX):
                act.wait_ge(x_loaded[k // KX], n * 16 + 16)
                nc.scalar.activation(x_hi[:, buf, k:k + KX], xstage[:, k:k + KX], ACT.Copy, scale=S_SCALE).then_inc(x_hi_ready, 1)

        def evict(act, n, m, first):
            q, j, c = gate_block(m)
            act.wait_ge(acc_ready, n * MB + m + 1)
            if j == 0 and not (first and q < 2):
                act.wait_ge(gi_stored[q % 2], n * (16 * PAIRS // 2) + 16 * (q // 2))
            nc.scalar.activation(out_stage[:, q % 2, :, j * COLS:(j + 1) * COLS],
                                 acc[m % BANKS][:].rearrange("p (s c) -> p s c", c=COLS), ACT.Identity,
                                 bias=bias_gi[:, c:c + 1], scale=UNSCALE).then_inc(acc_free, 1)
            if j == 5:
                act.wait_ge(acc_free, n * MB + (BANKS + m + 1))
                act.dma_start(gi_dram[bass.ds(n * BPOS, BPOS), :, q * GW:(q + 1) * GW].rearrange("s p f -> p s f"),
                              out_stage[:, q % 2]).then_inc(gi_stored[q % 2], 16)

        @block.scalar
        def _(act):
            act.sem_inc(acc_free, BANKS)
            split_w_hi(act, 0, 0)
            split_x_hi(act, 0, 0)
            split_w_hi(act, 1, 1)
            split_w_hi(act, 2, 2)
            act.wait_ge(bias_ready, 1)
            for m in range(MB):
                if m + 3 < MB:
                    split_w_hi(act, m + 3, m + 3)
                if m == 20:
                    act.wait_ge(slopes_summed, 1)
                    nc.scalar.activation(slope_sign[:], slope_sum[:], ACT.Sign).then_inc(sign_ready, 1)
                    split_x_hi(act, 1, 1)
                evict(act, 0, m, True)
            with act.Fori(1, NBLK - 1, 2) as n:
                for u in range(2):
                    for m in range(MB):
                        if m == 12:
                            split_x_hi(act, n + u + 1, u)
                        evict(act, n + u, m, False)
            for m in range(MB):
                evict(act, NBLK - 1, m, False)
                split_w_hi(act, MB + m, m)

        def split_w_lo(dve, j, m):
            dve.wait_ge(w_hi_ready, j + 1)
            c = gate_block(m)[2]
            nc.vector.scalar_tensor_tensor(out=w_lo[:, :, c * P:(c + 1) * P], in0=wstage[:, j % 2], scalar=W_SCALE,
                                           in1=w_hi[:, :, c * P:(c + 1) * P], op0=ALU.mult, op1=ALU.subtract)\
              .then_inc(w_lo_ready, 1)

        def split_x_lo(dve, n, buf):
            for k in range(0, KB, KX):
                dve.wait_ge(x_hi_ready, n * XPARTS + (k // KX + 1))
                nc.vector.scalar_tensor_tensor(out=x_lo[:, buf, k:k + KX], in0=xstage[:, k:k + KX], scalar=S_SCALE,
                                               in1=x_hi[:, buf, k:k + KX], op0=ALU.mult, op1=ALU.subtract)\
                  .then_inc(x_lo_ready, 1)

        @block.vector
        def _(dve):
            split_w_lo(dve, 0, 0)
            split_x_lo(dve, 0, 0)
            split_w_lo(dve, 1, 1)
            dve.wait_ge(bias_loaded, 32)
            nc.vector.tensor_copy(bias_gi[:, 2 * KB:MB], bias_i[:, 2 * KB:MB])
            nc.vector.tensor_copy(t["bias_hn"][:].rearrange("p q (c f) -> p (q c) f", f=COLS),
                                  bias_h[:, 2 * KB:MB].rearrange("p (b o) -> p b o", o=1).broadcast_to([P, KB, COLS]))
            nc.vector.tensor_tensor(bias_gi[:, 0:2 * KB], bias_i[:, 0:2 * KB], bias_h[:, 0:2 * KB], ALU.add)\
              .then_inc(bias_ready, 1)
            for m in range(2, MB):
                split_w_lo(dve, m, m)
            dve.wait_ge(slopes_loaded, 16)
            nc.vector.tensor_reduce(slope_sum[:], slope_rows[:], AX.X, ALU.add).then_inc(slopes_summed, 1)
            split_x_lo(dve, 1, 1)
            dve.wait_ge(rows_loaded, 7 * 16)
            nc.vector.tensor_tensor(t["gamma_s"][:], t["gamma_s"][:], sign_b[:], ALU.mult)
            nc.vector.tensor_tensor(t["beta_s"][:], t["beta_s"][:], sign_b[:], ALU.mult).then_inc(rows_ready, 1)
            with dve.Fori(1, NBLK - 1, 2) as n:
                for u in range(2):
                    split_x_lo(dve, n + u + 1, u)
            for m in range(MB):
                split_w_lo(dve, MB + m, m)
            nc.vector.memset(t["h"][:, :, 1], 0.0)
            nc.vector.memset(t["hp"][:, 1], 0.0)
            nc.vector.memset(t["flag"][:], 1)

        @block.tensor
        def _(pe):
            with pe.Fori(0, NBLK, 2) as n:
                for u in range(2):
                    for m in range(MB):
                        pe.wait_ge(w_lo_ready, m + 1)
                        pe.wait_ge(acc_free, n * MB + (u * MB + m + 1))
                        c = gate_block(m)[2]
                        for k in range(KB):
                            if m == 0 and k % KX == 0:
                                pe.wait_ge(x_lo_ready, n * XPARTS + (u * XPARTS + k // KX + 1))
                            hi = w_hi[:, k, c * P:(c + 1) * P]
                            lo = w_lo[:, k, c * P:(c + 1) * P]
                            nc.tensor.matmul(acc[m % BANKS][:], hi, x_hi[:, u, k], start=k == 0, stop=False)
                            nc.tensor.matmul(acc[m % BANKS][:], hi, x_lo[:, u, k], start=False, stop=False)
                            last = nc.tensor.matmul(acc[m % BANKS][:], lo, x_hi[:, u, k], start=False, stop=k == KB - 1)
                        last.then_inc(acc_ready, 1)


REC_X, REC_EXT, REC = NT, NT + SLICE, NT + SLICE + 2
ROW_SCALE, ROW_ID, ROW_EXT, ROW = 2 * SLICE, 2 * SLICE + 1, 2 * SLICE + 2, 2 * SLICE + 4
GROUPS = ((0, 2), (2, 3), (3, 4))
NG = len(GROUPS)


def split_exactly(engine, eng, parts, left, src, step):
    step(engine.tensor_copy(parts[0], src))
    step(engine.tensor_tensor(left[0], src, parts[0], ALU.subtract))
    step(engine.tensor_copy(parts[1], left[0]))
    step(engine.tensor_tensor(left[1], left[0], parts[1], ALU.subtract))
    return engine.tensor_copy(parts[2], left[1])


def recurrence(nc, ctx, t, gi_dram, sums_dram, states_dram, x_rows, y_rows, tables):
    def sb(name, shape, dt=F32):
        return ctx.enter_context(nc.sbuf_tensor(name, shape, dt))

    def pb(name, shape, dt=F32):
        return ctx.enter_context(nc.psum_tensor(name, shape, dt))

    def sem(name):
        return ctx.enter_context(nc.semaphore(name))

    w_hi, w_lo, h, hp, flag = t["w_hi"], t["w_lo"], t["h"], t["hp"], t["flag"]
    gi = sb("gi", [P, 2, PAIRS, GW])
    h_start = sb("h_start", [P, KB, COLS])
    gap_all = sb("gap_all", [P, KB, COLS - BATCH])
    gap = sb("gap", [P, 1])
    gap_over = sb("gap_over", [P, 1])
    gap_beyond = sb("gap_beyond", [P, 1])
    sums = sb("sums", [P, PAIRS, GW])
    rz_sum, hn = sums[:, :, 0:RZ], sums[:, :, RZ:GW]
    gi_n = sb("gi_n", [P, 2, PAIRS, 2 * COLS])
    warm_state = sb("warm_state", [P, 2, KB, COLS])
    warm_state_out = sb("warm_state_out", [P, KB, COLS])
    squares = warm_state_out
    diff_norm2 = sb("diff_norm2", [P, WARM_FULL + 1])
    diff_worst = sb("diff_worst", [P, 1])
    rz = sb("rz", [P, PAIRS, RZ])
    rn = sb("rn", [P, PAIRS, 2 * COLS])
    n_sum = sb("n_sum", [P, PAIRS, 2 * COLS])
    n_act = sb("n_act", [P, PAIRS, 2 * COLS])
    not_z = sb("not_z", [P, PAIRS, 2 * COLS])
    z_old = sb("z_old", [P, PAIRS, 2 * COLS])
    new_n = sb("new_n", [P, PAIRS, 2 * COLS])
    x_tile = sb("x_tile", [P, D])
    h_tok = sb("h_tok", [P, D])
    y_tile = sb("y_tile", [P, D])
    xhat = sb("xhat", [P, D])
    scaled = sb("scaled", [P, D])
    signed = sb("signed", [P, D])
    signs = sb("signs", [P, D], BF16)
    stats = sb("stats", [P, 2, 6])
    mean_var = sb("mean_var", [P, 2])
    var_eps = sb("var_eps", [P, 1])
    neg_mean = sb("neg_mean", [P, 1])
    rstd = sb("rstd", [P, 1])
    shift = sb("shift", [P, 1])
    scores = sb("scores", [P, NT])
    cscores = sb("cscores", [P, CLUSTERS])
    ckeys = sb("ckeys", [P, CLUSTERS])
    cbest = sb("cbest", [P, 1])
    chit = sb("chit", [P, CLUSTERS])
    tkeys_in = sb("tkeys_in", [P, NT])
    tkeys = sb("tkeys", [P, NT])
    tbest = sb("tbest", [P, 1])
    hit_t = sb("hit_t", [NT, P])
    record = sb("record", [P, REC])
    x_pick = sb("x_pick", [P, SLICE])
    x_scaled = sb("x_scaled", [P, SLICE])
    miss_big = sb("miss_big", [P, NT])
    cand = sb("cand", [P, 2, NT])
    curves, *curves_left = (a[0:NT, 0:2 * SLICE * GRID] for a in (xhat, scaled, signed))

    gates = pb("gates", [P, PAIRS, 512])
    h_turned = pb("h_turned", [P, D])
    hit_bank = pb("hit_bank", [P, 512])
    misc_bank = pb("misc_bank", [P, 512])
    affine = misc_bank[:, 0:2 * SLICE]

    gi_loaded, gi_n_loaded, warm_state_loaded = (
        [sem(f"{n}{i}") for i in range(2)] for n in ("gi_loaded", "gi_n_loaded", "warm_state_loaded"))
    sums_stored, warm_state_ready, warm_state_stored, diff_seen = (
        sem(n) for n in ("sums_stored", "warm_state_ready", "warm_state_stored", "diff_seen"))
    gates_ready, rz_sum_ready, rz_ready, not_z_ready, hn_ready, rn_ready, n_sum_ready, n_ready, z_old_ready, new_n_ready, h_ready = (
        sem(n) for n in ("gates_ready", "rz_sum_ready", "rz_ready", "not_z_ready", "hn_ready", "rn_ready", "n_sum_ready", "n_ready",
                         "z_old_ready", "new_n_ready", "h_ready"))
    head_ready, tail_ready = sem("head_ready"), sem("tail_ready")
    curves_loaded, split_step = sem("curves_loaded"), sem("split_step")
    start_step, start_copied, gap_step, gap_ready, gap_summed, pass_judged = (
        sem(n) for n in ("start_step", "start_copied", "gap_step", "gap_ready", "gap_summed", "pass_judged"))
    first_judged = sem("first_judged")
    x_loaded, y_ready, y_stored, turned, h_tok_ready, stats_ready, mean_ready, var_ready, rstd_ready, shift_ready = (
        sem(n) for n in ("x_tile_loaded", "y_ready", "y_stored", "turned", "h_tok_ready", "stats_ready", "mean_ready",
                         "var_ready", "rstd_ready", "shift_ready"))
    xhat_ready, scaled_ready, signed_ready, signs_ready, hit_ready, hit_turned, hit_t_ready, affine_ready = (
        sem(n) for n in ("xhat_ready", "scaled_ready", "signed_ready", "signs_ready", "hit_ready", "hit_turned",
                         "hit_t_ready", "affine_ready"))
    wait_carrier = sem("wait_carrier2")
    picked_ready, record_ready, record_kept, hit_kept = (sem(n) for n in ("picked_ready", "record_ready", "record_kept", "hit_kept"))
    route_step, slice_step = sem("route_step"), sem("slice_step")
    ROUTE_STEPS, SLICE_STEPS = 8, 9
    picked = scaled

    def groups_before(it, u):
        return it * (2 * NG) + u * NG

    def pair_of(p, i):
        return p * TILES + i + WARM // 2

    def diff_steps_of(it):
        return it * 2 - (pair_of(0, DIFF_TILE) * 2)

    def hit_wide():
        return record[:, 0:NT].rearrange("p (t o) -> p t o", o=1).broadcast_to([P, NT, SLICE])

    def sliced(ap):
        return ap[:].rearrange("p (t j) -> p t j", j=SLICE)

    def z_share(engine, u, g):
        a, b = GROUPS[g]
        return engine.tensor_tensor(z_old[:, a:b].rearrange("p q (c f) -> p q c f", c=2),
                                    rz[:, a:b, 2 * COLS:RZ].rearrange("p q (c f) -> p q c f", c=2),
                                    h[:, 2 * a:2 * b, 1 - u].rearrange("p (q c) f -> p q c f", c=2), ALU.mult)

    def passes(eng, body):
        body(0, True)
        eng.wait_ge(pass_judged, 1)
        eng.sem_inc(wait_carrier, 1)
        with eng.If(eng.value_load(flag[0:1, 0:1], min_val=0, max_val=P) > 0):
            with eng.Fori(1, CHUNKS + 1) as p:
                with eng.If(eng.value_load(flag[0:1, 0:1], min_val=0, max_val=P) > 0):
                    body(p, False)
                    eng.wait_ge(pass_judged, p + 1)
                    eng.sem_inc(wait_carrier, 1)

    FULL, HEADS, DIFFS = range(3)

    with nc.Block() as block:

        def pe_pairs(u, pairs, ks, mode):
            parts = hp[:, 1 - u]
            for q in pairs:
                out = gates[:, q]
                for k in ks:
                    for j in range(6):
                        c = (j // 2) * KB + 2 * q + j % 2
                        hi, lo = w_hi[:, k, c * P:(c + 1) * P], w_lo[:, k, c * P:(c + 1) * P]
                        o = out[:, j * COLS:(j + 1) * COLS]
                        last = nc.tensor.matmul(o, hi, parts[:, 1 if mode == DIFFS else 0, k], start=k == 0 and j == 0,
                                                stop=mode != FULL and k == KB - 1, skip_group_check=True)
                        if mode == FULL:
                            nc.tensor.matmul(o, hi, parts[:, 1, k], start=False, stop=False, skip_group_check=True)
                            last = nc.tensor.matmul(o, lo, parts[:, 0, k], start=False, stop=k == KB - 1, skip_group_check=True)
            return last

        def pe_step(pe, it, seeds, u, mode=FULL, after_state=None, after_first=None, after_second=None):
            before = groups_before(it, u) + seeds * NG
            state_ready = head_ready if mode == HEADS else tail_ready
            pe.wait_ge(state_ready, before - 2)
            pe_pairs(u, (0, 1), range(4), mode)
            pe.wait_ge(state_ready, before - 1)
            pe_pairs(u, (0, 1), (4, 5), mode)
            pe.wait_ge(state_ready, before)
            if after_state:
                after_state()
            pe_pairs(u, (0, 1), (6, 7), mode).then_inc(gates_ready, 1)
            if after_first:
                after_first()
            pe_pairs(u, (2,), range(KB), mode).then_inc(gates_ready, 1)
            if after_second:
                after_second()
            pe_pairs(u, (3,), range(KB), mode).then_inc(gates_ready, 1)

        def pe_turn():
            for k in range(KB):
                ins = nc.tensor.transpose(h_turned[:, k * P:(k + 1) * P], h[:, k].rearrange("p u f -> p (u f)"), t["ident"][:])
            ins.then_inc(turned, 1)

        def pe_hit(pe, T):
            pe.wait_ge(hit_ready, T)
            nc.tensor.transpose(hit_bank[0:REC, 0:P], record[:], t["ident"][:]).then_inc(hit_turned, 1)

        def pe_affine(pe, T):
            pe.wait_ge(hit_t_ready, T)
            nc.tensor.matmul(affine, hit_t[:], t["rows"][:, 0:2 * SLICE], start=True, stop=True).then_inc(affine_ready, 1)

        @block.tensor
        def _(pe):
            with pe.Fori(0, WARM_HEADS // 2) as it:
                for u in range(2):
                    pe_step(pe, it, 1, u, HEADS)
            with pe.Fori(WARM_HEADS // 2, WARM // 2) as it:
                for u in range(2):
                    pe_step(pe, it, 1, u)

            def one_pass(p, first):
                for u in range(2):
                    pe_step(pe, pair_of(p, 0), p + 2, u)
                with pe.Fori(1, DIFF_TILE - 1 if first else TILES) as i:
                    it, T = pair_of(p, i), p * TILES + i
                    pe_step(pe, it, p + 2, 0, after_state=pe_turn)
                    pe_step(pe, it, p + 2, 1, after_first=lambda: pe_hit(pe, T), after_second=lambda: pe_affine(pe, T))
                if first:
                    it = pair_of(0, DIFF_TILE - 1)
                    pe_step(pe, it, 2, 0, after_state=pe_turn)
                    pe_step(pe, it, 2, 1)
                    with pe.Fori(DIFF_TILE, TILES) as i:
                        it = pair_of(0, i)
                        pe_step(pe, it, 2, 0, DIFFS, after_first=pe_turn, after_second=lambda: pe_hit(pe, i - 1))
                        pe_affine(pe, i - 1)
                        pe_step(pe, it, 2, 1, DIFFS)
                pe.wait_ge(tail_ready, groups_before(pair_of(p, TILES), 0) + (p + 2) * NG)
                pe_turn()
                if first:
                    pe_hit(pe, TILES - 1)
                    pe_affine(pe, TILES - 1)
                pe.wait_ge(gap_ready, p + 1)
                nc.tensor.matmul(misc_bank[:, 64:65], t["ones"][:], gap_over[:], start=True, stop=True)\
                  .then_inc(gap_summed, 1)
                pe_hit(pe, p * TILES + TILES)
                pe_affine(pe, p * TILES + TILES)

            passes(pe, one_pass)

        SPREAD_DVE = "A0 B0 A1 C0 B1 T0 C1 T1 A2 B2 C2 T2".split()
        SPREAD_ACT = "A0 B0 A1 C0 B1 C1 A2 B2 C2".split()
        DENSE_DVE = "A0 B0 A1 C0 A2 B1 B2 C1 C2 T0 T1 T2".split()
        DENSE_ACT = "A0 B0 A1 C0 A2 B1 B2 C1 C2".split()
        LAST_DVE = "A0 B0 A1 C0 B1 D0 C1 D1 A2 B2 C2 D2".split()
        DIFFS_DVE = "A0 B0 A1 C0 D0 A2 B1 B2 C1 D1 C2 D2".split()
        DIFFS_ACT = "A0 B0 A1 A2 B1 B2".split()

        def act_stage(act, it, u, stage):
            g = int(stage[1])
            a, b = GROUPS[g]
            n = groups_before(it, u) + (g + 1)
            if stage[0] == "A":
                act.wait_ge(rz_sum_ready, n)
                nc.scalar.activation(rz[:, a:b], rz_sum[:, a:b], ACT.Sigmoid).then_inc(rz_ready, 1)
                nc.scalar.activation(not_z[:, a:b], rz_sum[:, a:b, 2 * COLS:RZ], ACT.Sigmoid, scale=-1.0)\
                  .then_inc(not_z_ready, 1)
            elif stage[0] == "B":
                act.wait_ge(n_sum_ready, n)
                nc.scalar.activation(n_act[:, a:b], n_sum[:, a:b], ACT.Tanh).then_inc(n_ready, 1)
            else:
                act.wait_ge(h_ready, n)
                nc.scalar.activation(hp[:, u, 0, 2 * a:2 * b], h[:, 2 * a:2 * b, u], ACT.Copy, scale=S_SCALE)\
                  .then_inc(head_ready, 1)

        def act_step(act, it, u, order=SPREAD_ACT, after={}):
            for stage in order:
                act_stage(act, it, u, stage)
                if stage in after:
                    after[stage]()

        def act_keep(act, it, u):
            act.wait_ge(h_ready, groups_before(it, u + 1))
            act.wait_ge(warm_state_stored, it * 32 + (u * 16 + 32 - WARM_HEADS * 16))
            nc.scalar.activation(warm_state_out[:], h[:, :, u], ACT.Copy, scale=S_SCALE).then_inc(warm_state_ready, 1)

        def act_diff(act, it, u):
            act.wait_ge(tail_ready, groups_before(it, u + 1) + 2 * NG)
            nc.scalar.activation(squares[:], hp[:, u, 1], ACT.Square,
                                 accum_out=diff_norm2[:, bass.ds(diff_steps_of(it) + (u + 1), 1)]).then_inc(diff_seen, 1)

        def act_h_tok(act, T):
            act.wait_ge(turned, T)
            act.wait_ge(y_ready, T)
            nc.scalar.activation(h_tok[:], h_turned[:], ACT.Copy).then_inc(h_tok_ready, 1)

        def act_normalise(act, T):
            act.wait_ge(shift_ready, T)
            nc.scalar.activation(xhat[:], h_tok[:], ACT.Identity, bias=shift[:], scale=rstd[:]).then_inc(xhat_ready, 1)

        def act_signs(act, T):
            act.wait_ge(signed_ready, T)
            nc.scalar.activation(signs[:], signed[:], ACT.Sign).then_inc(signs_ready, 1)

        def act_hit(act, T):
            act.wait_ge(hit_turned, T)
            nc.scalar.activation(hit_t[:], hit_bank[0:NT, 0:P], ACT.Copy).then_inc(hit_t_ready, 1)

        @block.scalar
        def _(act):
            act.sem_inc(head_ready, NG)
            with act.Fori(0, WARM_HEADS // 2) as it:
                for u in range(2):
                    act_step(act, it, u, DENSE_ACT)
            act_keep(act, WARM_HEADS // 2 - 1, 1)
            with act.Fori(WARM_HEADS // 2, WARM // 2) as it:
                for u in range(2):
                    act_step(act, it, u)
                    act_keep(act, it, u)

            def one_pass(p, first):
                act.wait_ge(start_copied, p + 1)
                nc.scalar.activation(hp[:, 1, 0], h[:, :, 1], ACT.Copy, scale=S_SCALE).then_inc(head_ready, NG)
                for u in range(2):
                    act_step(act, pair_of(p, 0), u)
                with act.Fori(1, DIFF_TILE - 1 if first else TILES) as i:
                    it, T = pair_of(p, i), p * TILES + i
                    act_h_tok(act, T)
                    act_step(act, it, 0, after={"A0": lambda: act_normalise(act, T), "C2": lambda: act_signs(act, T)})
                    act_step(act, it, 1, after={"A0": lambda: act_hit(act, T)})
                if first:
                    it, T = pair_of(0, DIFF_TILE - 1), DIFF_TILE - 1
                    act_h_tok(act, T)
                    act_step(act, it, 0, after={"A0": lambda: act_normalise(act, T), "C2": lambda: act_signs(act, T)})
                    act_step(act, it, 1)
                if first:
                    act.wait_ge(warm_state_stored, (WARM_FULL + 2) * 16)
                    act_diff(act, pair_of(0, DIFF_TILE - 1), 1)
                    with act.Fori(DIFF_TILE, TILES) as i:
                        it, T = pair_of(0, i), i
                        act_step(act, it, 0, DIFFS_ACT, {"B0": lambda: act_h_tok(act, T), "A1": lambda: act_hit(act, T - 1),
                                                         "B1": lambda: act_normalise(act, T)})
                        act_diff(act, it, 0)
                        act_step(act, it, 1, DIFFS_ACT, {"B2": lambda: act_signs(act, T)})
                        act_diff(act, it, 1)
                        act.sem_inc(head_ready, 2 * NG)
                T = p * TILES + TILES
                act_h_tok(act, T)
                if first:
                    act_hit(act, T - 1)
                act_normalise(act, T)
                act_signs(act, T)
                act_hit(act, T)

            passes(act, one_pass)

        def dve_stage(dve, it, seeds, u, stage, z_on_pool, from_diffs):
            g = int(stage[1])
            a, b = GROUPS[g]
            n = groups_before(it, u) + (g + 1)
            h_new = h[:, 2 * a:2 * b, u]

            def blocks(ap):
                return ap[:, a:b].rearrange("p q (c f) -> p (q c) f", c=2)

            if stage[0] == "A":
                dve.wait_ge(gates_ready, n)
                if g == 0:
                    dve.wait_ge(gi_loaded[u], it * 16 + 16)
                nc.vector.scalar_tensor_tensor(out=rz_sum[:, a:b], in0=gates[:, a:b, 0:RZ], scalar=UNSCALE,
                                               in1=gi[:, u, a:b, 0:RZ], op0=ALU.mult, op1=ALU.add).then_inc(rz_sum_ready, 1)
                base = gi[:, u, a:b, RZ:GW] if from_diffs else t["bias_hn"][:, a:b]
                nc.vector.scalar_tensor_tensor(out=hn[:, a:b], in0=gates[:, a:b, RZ:GW], scalar=UNSCALE, in1=base,
                                               op0=ALU.mult, op1=ALU.add).then_inc(hn_ready, 1)
            elif stage[0] == "B":
                dve.wait_ge(rz_ready, n)
                dve.wait_ge(hn_ready, n)
                nc.vector.tensor_tensor(rn[:, a:b], hn[:, a:b], rz[:, a:b, 0:2 * COLS], ALU.mult).then_inc(rn_ready, 1)
                dve.wait_ge(rn_ready, n)
                if from_diffs and g == 0:
                    dve.wait_ge(gi_n_loaded[u], diff_steps_of(it) * 8 + 16)
                nc.vector.tensor_tensor(n_sum[:, a:b], rn[:, a:b], gi_n[:, u, a:b] if from_diffs else gi[:, u, a:b, RZ:GW], ALU.add)\
                  .then_inc(n_sum_ready, 1)
                if not z_on_pool:
                    z_share(nc.vector, u, g).then_inc(z_old_ready, 1)
            elif stage[0] == "C":
                dve.wait_ge(not_z_ready, n)
                dve.wait_ge(n_ready, n)
                nc.vector.tensor_tensor(new_n[:, a:b], not_z[:, a:b], n_act[:, a:b], ALU.mult).then_inc(new_n_ready, 1)
                dve.wait_ge(z_old_ready, n)
                dve.wait_ge(new_n_ready, n)
                nc.vector.tensor_tensor(h_new, blocks(new_n), blocks(z_old), ALU.add).then_inc(h_ready, 1)
            elif stage[0] == "D":
                if g == 0:
                    dve.wait_ge(warm_state_loaded[u], diff_steps_of(it) * 8 + 16 * (1 + u))
                dve.wait_ge(h_ready, n)
                nc.vector.scalar_tensor_tensor(out=hp[:, u, 1, 2 * a:2 * b], in0=h_new, scalar=S_SCALE,
                                               in1=warm_state[:, u, 2 * a:2 * b], op0=ALU.mult, op1=ALU.subtract)\
                  .then_inc(tail_ready, 1)
            else:
                dve.wait_ge(head_ready, n + seeds * NG)
                nc.vector.scalar_tensor_tensor(out=hp[:, u, 1, 2 * a:2 * b], in0=h_new, scalar=S_SCALE,
                                               in1=hp[:, u, 0, 2 * a:2 * b], op0=ALU.mult, op1=ALU.subtract)\
                  .then_inc(tail_ready, 1)

        def dve_step(dve, it, seeds, u, order=SPREAD_DVE, z_on_pool=False, from_diffs=False, after={}):
            for stage in order:
                dve_stage(dve, it, seeds, u, stage, z_on_pool, from_diffs)
                if stage in after:
                    after[stage]()

        def dve_stats(dve, T):
            dve.wait_ge(h_tok_ready, T)
            for s in range(2):
                nc.vector.bn_stats(stats[:, s], h_tok[:, s * 512:(s + 1) * 512]).then_inc(stats_ready, 1)
            dve.wait_ge(stats_ready, T * 2)
            dve.sem_inc(wait_carrier, 1)
            nc.vector.bn_aggr(mean_var[:], stats[:].rearrange("p a b -> p (a b)")).then_inc(mean_ready, 1)
            dve.wait_ge(mean_ready, T)
            nc.vector.tensor_scalar(var_eps[:], mean_var[:, 1:2], LN_EPS, None, ALU.add)
            nc.vector.tensor_scalar(neg_mean[:], mean_var[:, 0:1], -1.0, None, ALU.mult).then_inc(var_ready, 1)

        def dve_route(dve, T):
            def step(ins, done):
                done[0] += 1
                ins.then_inc(route_step, 1)
                dve.wait_ge(route_step, T * ROUTE_STEPS + (done[0] - ROUTE_STEPS))
                return done[0]

            dve.wait_ge(signs_ready, T)
            done = [0]
            step(nc.vector.tensor_reduce(scores[:], sliced(signs), AX.X, ALU.add), done)
            step(nc.vector.tensor_reduce(cscores[:], scores[:].rearrange("p (c t) -> p c t", t=PER_CLUSTER), AX.X, ALU.add), done)
            step(nc.vector.scalar_tensor_tensor(out=ckeys[:], in0=cscores[:], scalar=float(CLUSTERS), in1=t["cramp"][:],
                                                op0=ALU.mult, op1=ALU.add), done)
            step(nc.vector.tensor_reduce(cbest[:], ckeys[:], AX.X, ALU.max), done)
            step(nc.vector.tensor_scalar(chit[:], ckeys[:], cbest[:], float(8 * NT * SLICE), ALU.is_equal, ALU.mult), done)
            step(nc.vector.scalar_tensor_tensor(out=tkeys_in[:], in0=scores[:], scalar=float(NT), in1=t["tramp"][:],
                                                op0=ALU.mult, op1=ALU.add), done)
            step(nc.vector.tensor_tensor(
                tkeys[:].rearrange("p (c t) -> p c t", t=PER_CLUSTER), tkeys_in[:].rearrange("p (c t) -> p c t", t=PER_CLUSTER),
                chit[:].rearrange("p (c o) -> p c o", o=1).broadcast_to([P, CLUSTERS, PER_CLUSTER]), ALU.add), done)
            assert step(nc.vector.tensor_reduce(tbest[:], tkeys[:], AX.X, ALU.max), done) == ROUTE_STEPS
            nc.vector.tensor_scalar(record[:, 0:NT], tkeys[:], tbest[:], None, ALU.is_equal).then_inc(hit_ready, 1)

        def dve_slice(dve, T):
            def step(ins, done):
                done[0] += 1
                ins.then_inc(slice_step, 1)
                dve.wait_ge(slice_step, T * SLICE_STEPS + (done[0] - SLICE_STEPS))
                return done[0]

            dve.wait_ge(picked_ready, T)
            done = [0]
            step(nc.vector.tensor_reduce(x_pick[:], picked[:].rearrange("p (t j) -> p j t", j=SLICE), AX.X, ALU.add), done)
            dve.wait_ge(affine_ready, T)
            step(nc.vector.tensor_tensor(x_scaled[:], x_pick[:], affine[:, 0:SLICE], ALU.mult), done)
            xs = record[:, REC_X:REC_EXT]
            step(nc.vector.tensor_tensor(xs, x_scaled[:], affine[:, SLICE:2 * SLICE], ALU.add), done)
            lo, hi = record[:, REC_EXT:REC_EXT + 1], record[:, REC_EXT + 1:REC]
            step(nc.vector.tensor_reduce(lo, xs, AX.X, ALU.min), done)
            step(nc.vector.tensor_reduce(hi, xs, AX.X, ALU.max), done)
            step(nc.vector.tensor_scalar(miss_big[:], record[:, 0:NT], 0.0, BIG, ALU.is_equal, ALU.mult), done)
            step(nc.vector.scalar_tensor_tensor(out=cand[:, 0], in0=record[:, 0:NT], scalar=lo, in1=miss_big[:],
                                                op0=ALU.mult, op1=ALU.add), done)
            step(nc.vector.scalar_tensor_tensor(out=cand[:, 1], in0=record[:, 0:NT], scalar=hi, in1=miss_big[:],
                                                op0=ALU.mult, op1=ALU.subtract), done)
            ext = t["extremes"]
            assert step(nc.vector.tensor_tensor(ext[:, 0], ext[:, 0], cand[:, 0], ALU.min), done) == SLICE_STEPS
            nc.vector.tensor_tensor(ext[:, 1], ext[:, 1], cand[:, 1], ALU.max).then_inc(record_ready, 1)

        @block.vector
        def _(dve):
            dve.sem_inc(tail_ready, NG)
            with dve.Fori(0, WARM_HEADS // 2) as it:
                for u in range(2):
                    dve_step(dve, it, 1, u, DENSE_DVE, z_on_pool=True)
            with dve.Fori(WARM_HEADS // 2, WARM // 2) as it:
                for u in range(2):
                    dve.wait_ge(sums_stored, it * 32 + (u * 16 + 16 - WARM_HEADS * 16))
                    dve_step(dve, it, 1, u)

            def one_pass(p, first):
                dve.wait_ge(tail_ready, groups_before(pair_of(p, 0), 0) + (p + 1) * NG)
                if first:
                    dve.wait_ge(sums_stored, (WARM_FULL + 1) * 16)
                    dve.wait_ge(warm_state_ready, WARM_FULL + 1)
                nc.vector.tensor_copy(h_start[:, :, BATCH:COLS], h[:, :, 1, 0:COLS - BATCH])
                nc.vector.tensor_copy(h_start[:, :, 0:BATCH], t["h0"][:])
                nc.vector.memset(t["extremes"][:, 0], BIG)
                nc.vector.memset(t["extremes"][:, 1], -BIG).then_inc(start_step, 1)
                dve.wait_ge(start_step, p + 1)
                nc.vector.tensor_copy(h[:, :, 1], h_start[:]).then_inc(start_copied, 1)
                dve.wait_ge(head_ready, groups_before(pair_of(p, 0), 0) + (p + 2) * NG)
                nc.vector.scalar_tensor_tensor(out=hp[:, 1, 1], in0=h[:, :, 1], scalar=S_SCALE, in1=hp[:, 1, 0],
                                               op0=ALU.mult, op1=ALU.subtract).then_inc(tail_ready, NG)
                for u in range(2):
                    dve_step(dve, pair_of(p, 0), p + 2, u)
                with dve.Fori(1, DIFF_TILE - 1 if first else TILES) as i:
                    it, T = pair_of(p, i), p * TILES + i
                    dve_stats(dve, T)
                    dve_step(dve, it, p + 2, 0)
                    dve_route(dve, T)
                    dve_step(dve, it, p + 2, 1)
                    dve_slice(dve, T)
                if first:
                    T = DIFF_TILE - 1
                    it = pair_of(0, T)
                    dve_stats(dve, T)
                    dve_step(dve, it, 2, 0)
                    dve_route(dve, T)
                    dve_step(dve, it, 2, 1, LAST_DVE)
                    with dve.Fori(DIFF_TILE, TILES) as i:
                        it, T = pair_of(0, i), i
                        dve_step(dve, it, 2, 0, DIFFS_DVE, from_diffs=True,
                                 after={"B0": lambda: dve.wait_ge(turned, T),
                                        "D0": lambda: dve_stats(dve, T)})
                        dve_slice(dve, T - 1)
                        dve_step(dve, it, 2, 1, DIFFS_DVE, from_diffs=True)
                        dve_route(dve, T)
                T = p * TILES + TILES
                dve_stats(dve, T)
                if first:
                    dve_slice(dve, T - 1)
                nc.vector.tensor_tensor(gap_all[:], h[:, :, 1, 0:COLS - BATCH], h_start[:, :, BATCH:COLS], ALU.subtract)\
                  .then_inc(gap_step, 1)
                dve.wait_ge(gap_step, p * 2 + 1)
                nc.vector.tensor_reduce(gap[:], gap_all[:], AX.XY, ALU.max, apply_absolute_value=True).then_inc(gap_step, 1)
                dve.wait_ge(gap_step, p * 2 + 2)
                if first:
                    dve.wait_ge(diff_seen, WARM_FULL + 1)
                    nc.vector.tensor_scalar(gap_beyond[:], gap[:], TOLERANCE, None, ALU.is_gt).then_inc(first_judged, 1)
                    nc.vector.tensor_reduce(diff_worst[:], diff_norm2[:], AX.X, ALU.max).then_inc(first_judged, 1)
                    dve.wait_ge(first_judged, 2)
                    nc.vector.scalar_tensor_tensor(out=gap_over[:], in0=diff_worst[:], scalar=(DIFF_BOUND * S_SCALE) ** 2,
                                                   in1=gap_beyond[:], op0=ALU.is_gt, op1=ALU.max).then_inc(gap_ready, 1)
                else:
                    nc.vector.tensor_scalar(gap_over[:], gap[:], TOLERANCE, None, ALU.is_gt).then_inc(gap_ready, 1)
                dve.wait_ge(gap_summed, p + 1)
                nc.vector.tensor_copy(flag[:], misc_bank[0:1, 64:65]).then_inc(pass_judged, 1)
                dve_route(dve, T)
                dve_slice(dve, T)
                dve.wait_ge(record_ready, T)

            passes(dve, one_pass)

        def pool_scale(pool, T):
            pool.wait_ge(var_ready, T)
            nc.gpsimd.tensor_tensor(rstd[:], var_eps[:], t["neg_half"][:], ALU.pow).then_inc(rstd_ready, 1)
            pool.wait_ge(rstd_ready, T)
            nc.gpsimd.tensor_tensor(shift[:], neg_mean[:], rstd[:], ALU.mult).then_inc(shift_ready, 1)

        def pool_tile(pool, T):
            pool.wait_ge(xhat_ready, T)
            nc.gpsimd.tensor_tensor(scaled[:], xhat[:], t["gamma_s"][:], ALU.mult).then_inc(scaled_ready, 1)
            pool.wait_ge(scaled_ready, T)
            nc.gpsimd.tensor_tensor(signed[:], scaled[:], t["beta_s"][:], ALU.add).then_inc(signed_ready, 1)
            pool.wait_ge(x_loaded, T * 16)
            pool.wait_ge(y_stored, T * 16)
            nc.gpsimd.tensor_tensor(y_tile[:], h_tok[:], x_tile[:], ALU.add).then_inc(y_ready, 1)
            pool.wait_ge(hit_ready, T)
            nc.gpsimd.tensor_tensor(sliced(picked), sliced(xhat), hit_wide(), ALU.mult).then_inc(picked_ready, 1)

        def pool_keep(pool, T, tile):
            pool.wait_ge(record_ready, T)
            nc.gpsimd.tensor_copy(t["records"][:, tile], record[:, REC_X:REC]).then_inc(record_kept, 1)
            nc.gpsimd.tensor_copy(t["hits_t"][:, tile], hit_t[:]).then_inc(hit_kept, 1)

        @block.gpsimd
        def _(pool):
            pool.sem_inc(y_ready, 1)
            with pool.Fori(0, WARM_HEADS // 2) as it:
                for u in range(2):
                    for g in range(NG):
                        pool.wait_ge(rz_ready, groups_before(it, u) + (g + 1))
                        z_share(nc.gpsimd, u, g).then_inc(z_old_ready, 1)

            done = [0]

            def step(ins):
                done[0] += 1
                ins.then_inc(split_step, 1)
                pool.wait_ge(split_step, done[0])

            pool.wait_ge(curves_loaded, 16)
            step(split_exactly(nc.gpsimd, pool, [t["curve_parts"][:, i] for i in range(3)],
                               curves_left, curves, step))

            def one_pass(p, first):
                with pool.Fori(0, DIFF_TILE - 2 if first else TILES) as i:
                    T = p * TILES + i + 1
                    pool_scale(pool, T)
                    pool_tile(pool, T)
                    pool_keep(pool, T, i)
                if first:
                    pool_scale(pool, DIFF_TILE - 1)
                    pool_tile(pool, DIFF_TILE - 1)
                    with pool.Fori(DIFF_TILE, TILES + 1) as T:
                        pool_scale(pool, T)
                        pool_keep(pool, T - 1, T - 2)
                        pool_tile(pool, T)
                    pool_keep(pool, TILES, TILES - 1)

            passes(pool, one_pass)

        def load_gi(sp, pos, u):
            sp.dma_start(gi[:, u].rearrange("p q f -> p (q f)"), gi_dram[bass.ds(pos, 1)].rearrange("o p f -> p (o f)"))\
              .then_inc(gi_loaded[u], 16)

        def gi_used(sp, it, u):
            sp.wait_ge(n_sum_ready, groups_before(it, u + 1))
            sp.sem_inc(wait_carrier, 1)

        def store_sums(sp, it, u):
            sp.wait_ge(rz_sum_ready, groups_before(it, u + 1))
            sp.wait_ge(hn_ready, groups_before(it, u + 1))
            sp.sem_inc(wait_carrier, 1)
            sp.dma_start(sums_dram[bass.ds(it * 2 + (u - WARM_HEADS), 1)].rearrange("o p f -> p (o f)"),
                         sums[:].rearrange("p q f -> p (q f)")).then_inc(sums_stored, 16)

        def store_state(sp, it, u):
            sp.wait_ge(warm_state_ready, it * 2 + (u + 2 - WARM_HEADS))
            sp.sem_inc(wait_carrier, 1)
            sp.dma_start(states_dram[bass.ds(it * 2 + (u + 1 - WARM_HEADS), 1)].rearrange("o p f -> p (o f)"),
                         warm_state_out[:].rearrange("p k f -> p (k f)")).then_inc(warm_state_stored, 16)

        def load_sums(sp, pos, u):
            sp.dma_start(gi[:, u].rearrange("p q f -> p (q f)"), sums_dram[bass.ds(pos - DIFF_FROM, 1)].rearrange("o p f -> p (o f)"))\
              .then_inc(gi_loaded[u], 16)
            sp.dma_start(gi_n[:, u], gi_dram[bass.ds(pos, 1)].rearrange("o p (q f) -> p (o q) f", q=PAIRS)[:, :, RZ:GW])\
              .then_inc(gi_n_loaded[u], 16)

        def load_state(sp, pos, u):
            sp.dma_start(warm_state[:, u].rearrange("p k f -> p (k f)"),
                         states_dram[bass.ds(pos - (DIFF_FROM - 1), 1)].rearrange("o p f -> p (o f)"))\
              .then_inc(warm_state_loaded[u], 16)

        def load_x(sp, tile):
            sp.dma_start(x_tile[:], x_rows[bass.ds(tile, 1)].rearrange("o p f -> p (o f)")).then_inc(x_loaded, 16)

        def store_y(sp, T, tile):
            sp.wait_ge(y_ready, T + 1)
            sp.sem_inc(wait_carrier, 1)
            sp.dma_start(y_rows[bass.ds(tile, 1)].rearrange("o p f -> p (o f)"), y_tile[:]).then_inc(y_stored, 16)

        @block.sync
        def _(sp):
            sp.sem_inc(y_stored, 16)
            sp.sem_inc(sums_stored, 16)
            sp.sem_inc(warm_state_stored, 16)
            load_gi(sp, LEN - WARM, 0)
            load_gi(sp, LEN - WARM + 1, 1)
            sp.dma_start(curves, tables.rearrange("t a f -> t (a f)")).then_inc(curves_loaded, 16)
            with sp.Fori(0, WARM_HEADS // 2) as it:
                for u in range(2):
                    gi_used(sp, it, u)
                    load_gi(sp, it * 2 + (LEN - WARM + 2 + u), u)
            store_state(sp, WARM_HEADS // 2 - 1, 1)
            with sp.Fori(WARM_HEADS // 2, WARM // 2 - 1) as it:
                for u in range(2):
                    store_sums(sp, it, u)
                    gi_used(sp, it, u)
                    load_gi(sp, it * 2 + (LEN - WARM + 2 + u), u)
                    store_state(sp, it, u)

            def one_pass(p, first):
                for u in range(2):
                    if first:
                        store_sums(sp, WARM // 2 - 1, u)
                    gi_used(sp, pair_of(p, -1), u)
                    load_gi(sp, u, u)
                    if first:
                        store_state(sp, WARM // 2 - 1, u)
                load_x(sp, 0)
                if first:
                    sp.wait_ge(sums_stored, (WARM_FULL + 1) * 16)
                    sp.wait_ge(warm_state_stored, (WARM_FULL + 2) * 16)
                    load_state(sp, DIFF_FROM - 1, 1)
                for u in range(2):
                    gi_used(sp, pair_of(p, 0), u)
                    load_gi(sp, 2 + u, u)
                with sp.Fori(1, DIFF_TILE - 1 if first else TILES - 1) as i:
                    it, T = pair_of(p, i), p * TILES + i
                    store_y(sp, T, i - 1)
                    load_x(sp, i)
                    for u in range(2):
                        gi_used(sp, it, u)
                        load_gi(sp, i * 2 + (2 + u), u)
                if first:
                    with sp.Fori(DIFF_TILE - 1, TILES - 1) as i:
                        for u in range(2):
                            gi_used(sp, pair_of(0, i), u)
                            load_sums(sp, i * 2 + (2 + u), u)
                            sp.wait_ge(tail_ready, groups_before(pair_of(0, i), u + 1) + 2 * NG)
                            sp.sem_inc(wait_carrier, 1)
                            load_state(sp, i * 2 + (2 + u), u)
                        store_y(sp, i, i - 1)
                        load_x(sp, i)
                for i in (TILES - 1, TILES):
                    store_y(sp, p * TILES + i, i - 1)
                    if i < TILES:
                        load_x(sp, i)
                sp.wait_ge(y_stored, p * (TILES * 16) + (TILES + 1) * 16)
                sp.sem_inc(wait_carrier, 1)

            passes(sp, one_pass)


def spline(nc, ctx, t, y_slices):
    def sb(name, shape, dt=F32):
        return ctx.enter_context(nc.sbuf_tensor(name, shape, dt))

    def sem(name):
        return ctx.enter_context(nc.semaphore(name))

    records, rows, hits_t, curve_parts = t["records"], t["rows"], t["hits_t"], t["curve_parts"]
    row_parts = sb("row_parts", [NT, 3, 4], BF16)
    row_left = sb("row_left", [NT, 2, 4])
    per_tok = sb("per_tok", [P, TILES, 4])
    span = sb("span", [P, TILES])
    span_eps = sb("span_eps", [P, TILES])
    rspan = sb("rspan", [P, TILES])
    off = sb("off", [P, TILES, SLICE])
    u_raw = sb("u_raw", [P, TILES, SLICE])
    u_clip = sb("u_clip", [P, TILES, SLICE])
    u_grid = sb("u_grid", [P, TILES, SLICE])
    near_i = sb("near_i", [P, TILES, SLICE], I32)
    near = sb("near", [P, TILES, SLICE])
    above = sb("above", [P, TILES, SLICE])
    cell = sb("cell", [P, TILES, SLICE])
    local = sb("local", [P, TILES, SLICE])
    RING = 8
    cell_off = sb("cell_off", [P, RING, SLICE, GRID])
    chosen = sb("chosen", [P, 3, 2, SLICE, GRID])
    curve = sb("curve", [P, TILES, 2, SLICE])
    rise = sb("rise", [P, TILES, SLICE])
    value = sb("value", [P, TILES, SLICE])
    delta = sb("delta", [P, TILES, SLICE])
    row_f = sb("row_f", [P, TILES])
    row_i = sb("row_i", [P, TILES], I32)

    turn_bank = ctx.enter_context(nc.psum_tensor("turn_bank", [P, 512], F32))
    tok_bank = [ctx.enter_context(nc.psum_tensor(f"tok_bank{i}", [P, 512], F32)) for i in range(2)]
    curve_bank = ctx.enter_context(nc.psum_tensor("curve_bank", [P, 4, 512], F32))

    SETS = ((0, 4), (4, 12), (12, 20), (20, 28), (28, 32))
    ADD_LAG = 8

    ext_turned, row_step, rows_split, tok_ready, tok_used, curve_ready, curve_used, cell_ready = (
        sem(n) for n in ("ext_turned", "row_step", "rows_split", "tok_ready", "tok_used", "curve_ready", "curve_used", "cell_ready"))
    math_step, cells_known, summed, delta_ready, added = (
        sem(n) for n in ("math_step", "cells_known", "summed", "delta_ready", "added"))

    with nc.Block() as block:

        @block.tensor
        def _(pe):
            for e in range(2):
                ins = nc.tensor.transpose(turn_bank[0:NT, e * P:(e + 1) * P], t["extremes"][:, e], t["ident"][:])
            ins.then_inc(ext_turned, 1)
            pe.wait_ge(rows_split, 1)

            def per_token(n):
                a, b = SETS[n]
                if n >= 2:
                    pe.wait_ge(tok_used, n - 1)
                for i in range(a, b):
                    for part in range(3):
                        ins = nc.tensor.matmul(tok_bank[n % 2][:, (i - a) * 4:(i - a + 1) * 4], hits_t[:, i], row_parts[:, part],
                                               start=part == 0, stop=part == 2)
                ins.then_inc(tok_ready, 1)

            per_token(0)
            for n, (a, b) in enumerate(SETS):
                if n + 1 < len(SETS):
                    per_token(n + 1)
                for i in range(a, b):
                    if i >= 4:
                        pe.wait_ge(curve_used, i - 3)
                    for part in range(3):
                        ins = nc.tensor.matmul(curve_bank[:, i % 4], hits_t[:, i], curve_parts[:, part],
                                               start=part == 0, stop=part == 2)
                    ins.then_inc(curve_ready, 1)

        @block.vector
        def _(dve):
            done = [0]

            def step(ins):
                done[0] += 1
                ins.then_inc(math_step, 1)
                dve.wait_ge(math_step, done[0])

            dve.wait_ge(ext_turned, 1)
            step(nc.vector.tensor_reduce(rows[:, ROW_EXT:ROW_EXT + 1], turn_bank[0:NT, 0:P], AX.X, ALU.min))
            step(nc.vector.tensor_reduce(rows[:, ROW_EXT + 1:ROW], turn_bank[0:NT, P:2 * P], AX.X, ALU.max))
            split_exactly(nc.vector, dve, [row_parts[:, i] for i in range(3)], [row_left[:, i] for i in range(2)],
                          rows[:, ROW_SCALE:ROW], step).then_inc(rows_split, 1)

            def wide(ap):
                return ap.rearrange("p (i o) -> p i o", o=1).broadcast_to([P, ap.shape[1], SLICE])

            def cells(n):
                a, b = SETS[n]
                s = slice(a, b)
                scale, tile_id, low, high = (per_tok[:, s, f] for f in range(4))
                dve.wait_ge(tok_ready, n + 1)
                nc.vector.tensor_copy(per_tok[:, s], tok_bank[n % 2][:, 0:4 * (b - a)].rearrange("p (i f) -> p i f", f=4))\
                  .then_inc(tok_used, 1)
                dve.wait_ge(tok_used, n + 1)
                step(nc.vector.tensor_tensor(span[:, s], high, low, ALU.subtract))
                step(nc.vector.tensor_scalar(span_eps[:, s], span[:, s], 1e-8, None, ALU.add))
                step(nc.vector.tensor_tensor(off[:, s], records[:, s, 0:SLICE], wide(low), ALU.subtract))
                step(nc.vector.reciprocal(rspan[:, s], span_eps[:, s]))
                step(nc.vector.tensor_tensor(u_raw[:, s], off[:, s], wide(rspan[:, s]), ALU.mult))
                step(nc.vector.tensor_scalar(u_clip[:, s], u_raw[:, s], 0.0, 1.0 - 1e-6, ALU.max, ALU.min))
                step(nc.vector.tensor_scalar(u_grid[:, s], u_clip[:, s], float(GRID), None, ALU.mult))
                step(nc.vector.tensor_copy(near_i[:, s], u_grid[:, s]))
                step(nc.vector.tensor_copy(near[:, s], near_i[:, s]))
                step(nc.vector.tensor_tensor(above[:, s], near[:, s], u_grid[:, s], ALU.is_gt))
                nc.vector.tensor_tensor(cell[:, s], near[:, s], above[:, s], ALU.subtract).then_inc(cells_known, 1)
                dve.wait_ge(cells_known, n + 1)
                step(nc.vector.tensor_tensor(local[:, s], u_grid[:, s], cell[:, s], ALU.subtract))
                step(nc.vector.tensor_tensor(row_f[:, s], tile_id, t["token_row"][:, s], ALU.add))
                step(nc.vector.tensor_copy(row_i[:, s], row_f[:, s]))

            def choose(i):
                dve.wait_ge(cell_ready, i + 1)
                dve.wait_ge(curve_ready, i + 1)
                away = cell_off[:, i % RING].rearrange("p j g -> p (j g)").rearrange("p (o f) -> p o f", o=1)
                nc.vector.scalar_tensor_tensor(
                    out=chosen[:, i % 3].rearrange("p a j g -> p a (j g)"), in0=away.broadcast_to([P, 2, SLICE * GRID]),
                    scalar=0.0, in1=curve_bank[:, i % 4].rearrange("p (a f) -> p a f", a=2), op0=ALU.is_equal, op1=ALU.mult)\
                  .then_inc(curve_used, 1)

            cells(0)
            choose(0)
            for n, (a, b) in enumerate(SETS):
                if n + 1 < len(SETS):
                    cells(n + 1)
                for i in range(a, b):
                    if i >= 2:
                        dve.wait_ge(summed, i - 1)
                    if i + 1 < TILES:
                        choose(i + 1)
                    dve.wait_ge(curve_used, i + 1)
                    nc.vector.tensor_reduce(curve[:, i], chosen[:, i % 3], AX.X, ALU.add).then_inc(summed, 1)
                dve.wait_ge(summed, b)
                s = slice(a, b)
                step(nc.vector.tensor_tensor(rise[:, s], curve[:, s, 1], local[:, s], ALU.mult))
                step(nc.vector.tensor_tensor(value[:, s], curve[:, s, 0], rise[:, s], ALU.add))
                nc.vector.tensor_tensor(delta[:, s], value[:, s], wide(per_tok[:, s, 0]), ALU.mult).then_inc(delta_ready, 1)

        @block.gpsimd
        def _(pool):
            def add(i):
                for n, (a, b) in enumerate(SETS):
                    if i == a:
                        pool.wait_ge(delta_ready, n + 1)
                pool.indirect_dma_start(out=y_slices[:], out_offset=bass.IndirectOffsetOnAxis(ap=row_i[:, i:i + 1], axis=0),
                                        in_=delta[:, i], in_offset=None, compute_op=ALU.add).then_inc(added, 16)

            for i in range(TILES):
                for n, (a, b) in enumerate(SETS):
                    if i == a:
                        pool.wait_ge(cells_known, n + 1)
                if i >= RING:
                    pool.wait_ge(curve_used, i - RING + 1)
                nc.gpsimd.tensor_tensor(
                    cell_off[:, i % RING], cell[:, i].rearrange("p (j o) -> p j o", o=1).broadcast_to([P, SLICE, GRID]),
                    t["grid_ramp"][:].rearrange("p (o g) -> p o g", o=1).broadcast_to([P, SLICE, GRID]), ALU.subtract)\
                  .then_inc(cell_ready, 1)
                if i >= ADD_LAG:
                    add(i - ADD_LAG)
            for i in range(TILES - ADD_LAG, TILES):
                add(i)
            pool.wait_ge(added, 16 * TILES)


def constants(nc, t):
    made = t["const_made"]
    with nc.Block() as block:
        @block.gpsimd
        def _(pool):
            nc.gpsimd.memset(t["ident"][:], 0.0).then_inc(made, 1)
            pool.wait_ge(made, 1)
            nc.gpsimd.affine_select(out=t["ident"][:], in_=t["ident"][:], compare_op=ALU.not_equal, fill=1.0, base=0,
                                    pattern=[[-1, P]], channel_multiplier=1)
            nc.gpsimd.memset(t["ones"][:], 1.0)
            nc.gpsimd.memset(t["neg_half"][:], -0.5)
            nc.gpsimd.iota(t["cramp"][:], pattern=[[-1, CLUSTERS]], base=CLUSTERS - 1, channel_multiplier=0,
                           allow_small_or_imprecise_dtypes=True)
            nc.gpsimd.iota(t["tramp"][:], pattern=[[-1, NT]], base=NT - 1, channel_multiplier=0,
                           allow_small_or_imprecise_dtypes=True)
            nc.gpsimd.iota(t["grid_ramp"][:], pattern=[[1, GRID]], base=0, channel_multiplier=0,
                           allow_small_or_imprecise_dtypes=True)
            nc.gpsimd.iota(t["token_row"][:], pattern=[[P * NT, TILES]], base=0, channel_multiplier=NT,
                           allow_small_or_imprecise_dtypes=True)
            nc.gpsimd.iota(t["rows"][:, ROW_ID:ROW_ID + 1], pattern=[[0, 1]], base=0, channel_multiplier=1,
                           allow_small_or_imprecise_dtypes=True)


def program(nc, xT, x_rows, h0, W_ih, W_hh, b_ih, b_hh, gamma, beta, gamma_t, beta_t, slopes, tables, out_scale, y):
    gi_dram = nc.dram_tensor("gi_scratch", [LEN, P, PAIRS * GW], F32, kind="Internal").ap()
    sums_dram = nc.dram_tensor("sums_scratch", [WARM_FULL, P, PAIRS * GW], F32, kind="Internal").ap()
    states_dram = nc.dram_tensor("states_scratch", [WARM_FULL + 1, P, KB * COLS], F32, kind="Internal").ap()
    sign_dram = nc.dram_tensor("sign_scratch", [NT, SLICE], F32, kind="Internal").ap()
    with ExitStack() as ctx:
        shapes = {
            "w_hi": ([P, KB, 3 * D], F16), "w_lo": ([P, KB, 3 * D], F16),
            "h": ([P, KB, 2, COLS], F32),
            "hp": ([P, 2, 2, KB, COLS], F16),
            "h0": ([P, KB, BATCH], F32), "flag": ([1, 1], I32), "bias_hn": ([P, PAIRS, 2 * COLS], F32),
            "gamma_s": ([P, D], F32), "beta_s": ([P, D], F32),
            "ident": ([P, P], F32), "ones": ([P, P], F32), "neg_half": ([P, 1], F32),
            "cramp": ([P, CLUSTERS], F32), "tramp": ([P, NT], F32), "grid_ramp": ([P, GRID], F32),
            "token_row": ([P, TILES], F32), "rows": ([NT, ROW], F32),
        }
        t = {n: ctx.enter_context(nc.sbuf_tensor(n, s, d)) for n, (s, d) in shapes.items()}
        t["const_made"] = ctx.enter_context(nc.semaphore("const_made"))
        constants(nc, t)
        with ExitStack() as phase:
            input_product(nc, phase, t, W_ih, W_hh, b_ih, b_hh, xT, gi_dram, slopes, gamma, beta, gamma_t, beta_t,
                          out_scale, h0, sign_dram)
        t["records"] = ctx.enter_context(nc.sbuf_tensor("records", [P, TILES, REC - REC_X], F32))
        t["hits_t"] = ctx.enter_context(nc.sbuf_tensor("hits_t", [NT, TILES, P], BF16))
        t["curve_parts"] = ctx.enter_context(nc.sbuf_tensor("curve_parts", [NT, 3, 2 * SLICE * GRID], BF16))
        t["extremes"] = ctx.enter_context(nc.sbuf_tensor("extremes", [P, 2, NT], F32))
        with ExitStack() as phase:
            recurrence(nc, phase, t, gi_dram, sums_dram, states_dram, x_rows, y.rearrange("(i p) f -> i p f", p=P), tables)
        with ExitStack() as phase:
            spline(nc, phase, t, y.rearrange("r (t j) -> (r t) j", j=SLICE))


def kernel(x, cond_2048, L0_cond_W_ih, L0_cond_W_hh, L0_cond_b_ih, L0_cond_b_hh, L0_ffn_ln_gamma, L0_ffn_ln_beta,
           L0_ffn_spline_bases, L0_ffn_spline_slopes, L0_ffn_output_scale):
    import numpy as np
    import concourse.bacc as bacc
    from concourse.bass_utils import run_bass_kernel_spmd

    def lay(a):
        return np.ascontiguousarray(a)

    x = np.asarray(x)
    steps = x.reshape(BATCH, CHUNKS, LEN, D)
    arrays = {
        "xT": lay(steps.transpose(3, 2, 1, 0).reshape(D, TOKENS)),
        "x_rows": lay(steps.transpose(2, 1, 0, 3).reshape(TILES, P, D)),
        "h0": lay(np.asarray(cond_2048).reshape(BATCH, KB, P).transpose(2, 1, 0)),
        "W_ih": lay(L0_cond_W_ih), "W_hh": lay(L0_cond_W_hh),
        "b_ih": lay(np.asarray(L0_cond_b_ih).reshape(MB, P).T), "b_hh": lay(np.asarray(L0_cond_b_hh).reshape(MB, P).T),
        "gamma": lay(np.asarray(L0_ffn_ln_gamma).reshape(1, D)), "beta": lay(np.asarray(L0_ffn_ln_beta).reshape(1, D)),
        "gamma_t": lay(np.asarray(L0_ffn_ln_gamma).reshape(NT, SLICE)),
        "beta_t": lay(np.asarray(L0_ffn_ln_beta).reshape(NT, SLICE)),
        "slopes": lay(np.asarray(L0_ffn_spline_slopes).reshape(NT, SLICE * GRID)),
        "tables": lay(np.stack([np.asarray(L0_ffn_spline_bases).reshape(NT, -1),
                                np.asarray(L0_ffn_spline_slopes).reshape(NT, -1)], axis=1)),
        "out_scale": lay(np.asarray(L0_ffn_output_scale).reshape(NT, 1)),
    }
    nc = bacc.Bacc("TRN2", target_bir_lowering=False, num_devices=1)
    args = [nc.dram_tensor(f"in_{n}", a.shape, mybir.dt.from_np(a.dtype), kind="ExternalInput").ap() for n, a in arrays.items()]
    y = nc.dram_tensor("y", (TOKENS, D), F32, kind="ExternalOutput").ap()
    program(nc, *args, y)
    got = run_bass_kernel_spmd(nc, [{f"in_{n}": a for n, a in arrays.items()}], core_ids=[0]).results[0]["y"]
    return lay(np.asarray(got).reshape(LEN, CHUNKS, BATCH, D).transpose(2, 1, 0, 3).reshape(BATCH, SEQ, D))
```
